# Optimizing a Trainium2 kernel written in Bass

```python
import numpy as np
import jax
import jax.numpy as jnp

def _softmax(x, axis=-1):
    return jax.nn.softmax(x, axis=axis)

def _gelu(x):
    return jax.nn.gelu(x, approximate=True)

def _silu(x):
    return jax.nn.silu(x)

def _sigmoid(x):
    return jax.nn.sigmoid(x)

def _layernorm(x, axis=-1, eps=1e-05):
    m = jnp.mean(x, axis=axis, keepdims=True)
    v = jnp.var(x, axis=axis, keepdims=True)
    return (x - m) / jnp.sqrt(v + eps)

def _scatter_add(tgt, idx, src, axis=0):
    return tgt.at[idx].add(src)

def _segment_sum(src, seg, n):
    return jax.ops.segment_sum(src, seg, n)
kernel_name = 'mk_decoder_preln_d2_seqx_r4_bcd0ab'

def setup_inputs(seed: int=0):
    np.random.seed(seed)
    _w = jnp.asarray

    def _rec_inputs():
        import jax
        import jax.numpy as jnp
        _rk = jax.random.key(seed)
        x = 7.22e-05 + 1 * jax.random.normal(jax.random.fold_in(_rk, 1), (16, 256, 256), jnp.float32)
        _lenS = 256 - jax.random.randint(jax.random.fold_in(_rk, 7), (16,), 0, max(1, 256 // 4) + 1, jnp.int32)
        _lenS2 = 256 - jax.random.randint(jax.random.fold_in(_rk, 8), (16,), 0, max(1, 256 // 4) + 1, jnp.int32)
        _ctx_1024P = jax.random.normal(jax.random.fold_in(_rk, 11), (16, 16, 256), jnp.float32)
        _ctx_1024c = jax.random.dirichlet(jax.random.fold_in(_rk, 511), 0.3 * jnp.ones((16,), jnp.float32), (16, 256))
        _ctx_1024t = jnp.einsum('bsk,bkd->bsd', _ctx_1024c, _ctx_1024P)
        _ctx_1024t = _ctx_1024t * jax.lax.rsqrt(jnp.mean(jnp.square(_ctx_1024t)) + 1e-12) * 0.953939
        ctx_1024 = 4.13588e-05 + 0.999923 * (_ctx_1024t + 0.3 * jax.random.normal(jax.random.fold_in(_rk, 611), (16, 256, 256), jnp.float32))
        _validS = jnp.arange(256)[None, :] < _lenS[:, None]
        _validS2 = jnp.arange(256)[None, :] < _lenS2[:, None]
        _causal = jnp.tril(jnp.ones((256, 256), dtype=bool))
        mask_Bx1x1xS2_fk0 = jnp.where(jnp.broadcast_to(_validS2[:, None, None, :], (16, 1, 1, 256)), 0.0, 1.0).astype(jnp.float32)
        return (x, ctx_1024, mask_Bx1x1xS2_fk0)
    x, ctx_1024, mask_Bx1x1xS2_fk0 = _rec_inputs()

    def _L0_attn_setup():
        import jax, jax.numpy as jnp
        import numpy as np
        BASE_THETA = 0.5
        K_DOP = 0.2
        K_NOR = 0.15
        K_SERO = 0.1
        DIM = 256
        key = jax.random.key(seed)
        ks = jax.random.split(key, 9)
        scale = 1.0 / np.sqrt(DIM)
        x = jax.random.normal(ks[0], (2, 512, DIM), dtype=jnp.float32)
        Wq = jax.random.normal(ks[1], (DIM, DIM), dtype=jnp.float32) * scale
        bq = jnp.zeros((DIM,), dtype=jnp.float32)
        Wk = jax.random.normal(ks[2], (DIM, DIM), dtype=jnp.float32) * scale
        bk = jnp.zeros((DIM,), dtype=jnp.float32)
        Wv = jax.random.normal(ks[3], (DIM, DIM), dtype=jnp.float32) * scale
        bv = jnp.zeros((DIM,), dtype=jnp.float32)
        Wo = jax.random.normal(ks[4], (DIM, DIM), dtype=jnp.float32) * scale
        bo = jnp.zeros((DIM,), dtype=jnp.float32)
        return {'x': x, 'Wq': Wq, 'bq': bq, 'Wk': Wk, 'bk': bk, 'Wv': Wv, 'bv': bv, 'Wo': Wo, 'bo': bo}
    _L0_attn_all = _L0_attn_setup()
    _L0_attn_in = {k: v for k, v in _L0_attn_all.items() if k in ('Wq', 'bq', 'Wk', 'bk', 'Wv', 'bv', 'Wo', 'bo')}
    del _L0_attn_all

    def _L0_xattn_setup():
        import jax, jax.numpy as jnp
        import numpy as np
        H, D, DIM = (8, 128, 256)
        QB, N = (16, 128)

        def layer_norm(x, g, b, eps=1e-05):
            mu = x.mean(-1, keepdims=True)
            var = ((x - mu) ** 2).mean(-1, keepdims=True)
            return (x - mu) / jnp.sqrt(var + eps) * g + b
        key = jax.random.key(seed)
        ks = jax.random.split(key, 8)
        rn = lambda k, shape, s=1.0: jax.random.normal(k, shape, jnp.float32) * s
        return {'q': rn(ks[0], (QB, N, DIM)), 'k': rn(ks[1], (QB, N, DIM)), 'v': rn(ks[2], (QB, N, DIM)), 'ln_g': jnp.ones(DIM, jnp.float32), 'ln_b': jnp.zeros(DIM, jnp.float32), 'w_in': rn(ks[3], (H * D, DIM), 0.02), 'wp_w1': rn(ks[4], (D, 2 * D), 0.05), 'wp_b1': jnp.zeros(D, jnp.float32), 'wp_ln_g': jnp.ones(D, jnp.float32), 'wp_ln_b': jnp.zeros(D, jnp.float32), 'wp_w2': rn(ks[5], (3, D), 0.05), 'wp_b2': jnp.zeros(3, jnp.float32), 'w_out': rn(ks[6], (DIM, H * D), 0.02), 'b_out': jnp.zeros(DIM, jnp.float32)}
    _L0_xattn_all = _L0_xattn_setup()
    _L0_xattn_in = {k: v for k, v in _L0_xattn_all.items() if k in ('ln_g', 'ln_b', 'w_in', 'wp_w1', 'wp_b1', 'wp_ln_g', 'wp_ln_b', 'wp_w2', 'wp_b2', 'w_out', 'b_out')}
    del _L0_xattn_all

    def _L0_ffn_setup():
        import jax, jax.numpy as jnp
        import numpy as np
        B, S, H, E, K, I = (4, 512, 256, 8, 2, 1024)
        GATE_EPS = 1e-06
        LN_EPS = 1e-05
        key = jax.random.key(seed)
        k0, k1, k2, k3 = jax.random.split(key, 4)
        x = jax.random.normal(k0, (B, S, H), jnp.float32)
        gate_w = jax.random.normal(k1, (E, H), jnp.float32) * np.float32(np.sqrt(2.0 / (H + E)))
        expert_bias = jnp.zeros((E,), jnp.float32)
        w_up = jax.random.normal(k2, (E, I, H), jnp.float32) * np.float32(np.sqrt(2.0 / (H + I)))
        w_down = jax.random.normal(k3, (E, H, I), jnp.float32) * np.float32(np.sqrt(2.0 / (H + I)))
        return {'x': x, 'gate_w': gate_w, 'expert_bias': expert_bias, 'w_up': w_up, 'w_down': w_down}
    _L0_ffn_all = _L0_ffn_setup()
    _L0_ffn_in = {k: v for k, v in _L0_ffn_all.items() if k in ('gate_w', 'expert_bias', 'w_up', 'w_down')}
    del _L0_ffn_all

    def _L1_attn_setup():
        import jax, jax.numpy as jnp
        import numpy as np
        NUM_HEADS = 16
        HIDDEN = 256
        ATTN_DIM = 64
        HEAD_OUT = 64
        OUT_DIM = 256
        BATCH, SEQ = (2, 512)

        def _split_heads(y, h):
            b, s, _ = y.shape
            return y.reshape(b, s, h, -1).transpose(0, 2, 1, 3)
        key = jax.random.key(seed)
        ks = jax.random.split(key, 9)
        s_in = 1.0 / np.sqrt(HIDDEN)
        s_o = 1.0 / np.sqrt(NUM_HEADS * HEAD_OUT)
        return {'x': jax.random.normal(ks[0], (BATCH, SEQ, HIDDEN), dtype=jnp.float32), 'Wq': jax.random.uniform(ks[1], (HIDDEN, NUM_HEADS * ATTN_DIM), jnp.float32, -s_in, s_in), 'bq': jax.random.uniform(ks[2], (NUM_HEADS * ATTN_DIM,), jnp.float32, -s_in, s_in), 'Wk': jax.random.uniform(ks[3], (HIDDEN, NUM_HEADS * ATTN_DIM), jnp.float32, -s_in, s_in), 'bk': jax.random.uniform(ks[4], (NUM_HEADS * ATTN_DIM,), jnp.float32, -s_in, s_in), 'Wv': jax.random.uniform(ks[5], (HIDDEN, NUM_HEADS * HEAD_OUT), jnp.float32, -s_in, s_in), 'bv': jax.random.uniform(ks[6], (HIDDEN, NUM_HEADS * HEAD_OUT)[1:], jnp.float32, -s_in, s_in), 'Wo': jax.random.uniform(ks[7], (NUM_HEADS * HEAD_OUT, OUT_DIM), jnp.float32, -s_o, s_o), 'bo': jax.random.uniform(ks[8], (OUT_DIM,), jnp.float32, -s_o, s_o)}
    _L1_attn_all = _L1_attn_setup()
    _L1_attn_in = {k: v for k, v in _L1_attn_all.items() if k in ('Wq', 'bq', 'Wk', 'bk', 'Wv', 'bv', 'Wo', 'bo')}
    del _L1_attn_all

    def _L1_xattn_setup():
        import jax, jax.numpy as jnp
        import numpy as np
        DIM, HEADS = (256, 16)
        B, S = (4, 512)
        HD = DIM // HEADS
        key = jax.random.key(seed)
        ks = jax.random.split(key, 8)
        scale = 1.0 / np.sqrt(DIM)
        q = jax.random.normal(ks[0], (B, S, DIM), jnp.float32)
        k = jax.random.normal(ks[1], (B, S, DIM), jnp.float32)
        v = jax.random.normal(ks[2], (B, S, DIM), jnp.float32)
        mask = jax.random.bernoulli(ks[3], 0.1, (B, 1, 1, S)).astype(jnp.float32)
        Wq = jax.random.normal(ks[4], (DIM, DIM), jnp.float32) * scale
        Wk = jax.random.normal(ks[5], (DIM, DIM), jnp.float32) * scale
        Wv = jax.random.normal(ks[6], (DIM, DIM), jnp.float32) * scale
        Wo = jax.random.normal(ks[7], (DIM, DIM), jnp.float32) * scale
        return {'q': q, 'k': k, 'v': v, 'mask': mask, 'Wq': Wq, 'Wk': Wk, 'Wv': Wv, 'Wo': Wo}
    _L1_xattn_all = _L1_xattn_setup()
    _L1_xattn_in = {k: v for k, v in _L1_xattn_all.items() if k in ('Wq', 'Wk', 'Wv', 'Wo')}
    del _L1_xattn_all

    def _L1_ffn_setup():
        import jax, jax.numpy as jnp
        import numpy as np
        B, S, D, O, E = (8, 1024, 256, 256, 64)
        key = jax.random.key(seed)
        kx, kgw, kgb, kew, keb = jax.random.split(key, 5)
        x = jax.random.normal(kx, (B, S, D), dtype=jnp.float32)
        gate_w = jax.random.normal(kgw, (E, D), dtype=jnp.float32) * 0.02
        gate_b = jnp.zeros((E,), dtype=jnp.float32)
        expert_w = jax.random.normal(kew, (E, D, O), dtype=jnp.float32) * 0.02
        expert_b = jnp.zeros((E, O), dtype=jnp.float32)
        return {'x': x, 'gate_w': gate_w, 'gate_b': gate_b, 'expert_w': expert_w, 'expert_b': expert_b}
    _L1_ffn_all = _L1_ffn_setup()
    _L1_ffn_in = {k: v for k, v in _L1_ffn_all.items() if k in ('gate_w', 'gate_b', 'expert_w', 'expert_b')}
    del _L1_ffn_all
    return {'x': x, 'ctx_1024': ctx_1024, 'mask_Bx1x1xS2_fk0': mask_Bx1x1xS2_fk0, 'L0_attn_Wq': _L0_attn_in['Wq'], 'L0_attn_bq': _L0_attn_in['bq'], 'L0_attn_Wk': _L0_attn_in['Wk'], 'L0_attn_bk': _L0_attn_in['bk'], 'L0_attn_Wv': _L0_attn_in['Wv'], 'L0_attn_bv': _L0_attn_in['bv'], 'L0_attn_Wo': _L0_attn_in['Wo'], 'L0_attn_bo': _L0_attn_in['bo'], 'L0_xattn_ln_g': _L0_xattn_in['ln_g'], 'L0_xattn_ln_b': _L0_xattn_in['ln_b'], 'L0_xattn_w_in': _L0_xattn_in['w_in'], 'L0_xattn_wp_w1': _L0_xattn_in['wp_w1'], 'L0_xattn_wp_b1': _L0_xattn_in['wp_b1'], 'L0_xattn_wp_ln_g': _L0_xattn_in['wp_ln_g'], 'L0_xattn_wp_ln_b': _L0_xattn_in['wp_ln_b'], 'L0_xattn_wp_w2': _L0_xattn_in['wp_w2'], 'L0_xattn_wp_b2': _L0_xattn_in['wp_b2'], 'L0_xattn_w_out': _L0_xattn_in['w_out'], 'L0_xattn_b_out': _L0_xattn_in['b_out'], 'L0_ffn_gate_w': _L0_ffn_in['gate_w'], 'L0_ffn_expert_bias': _L0_ffn_in['expert_bias'], 'L0_ffn_w_up': _L0_ffn_in['w_up'], 'L0_ffn_w_down': _L0_ffn_in['w_down'], 'L1_attn_Wq': _L1_attn_in['Wq'], 'L1_attn_bq': _L1_attn_in['bq'], 'L1_attn_Wk': _L1_attn_in['Wk'], 'L1_attn_bk': _L1_attn_in['bk'], 'L1_attn_Wv': _L1_attn_in['Wv'], 'L1_attn_bv': _L1_attn_in['bv'], 'L1_attn_Wo': _L1_attn_in['Wo'], 'L1_attn_bo': _L1_attn_in['bo'], 'L1_xattn_Wq': _L1_xattn_in['Wq'], 'L1_xattn_Wk': _L1_xattn_in['Wk'], 'L1_xattn_Wv': _L1_xattn_in['Wv'], 'L1_xattn_Wo': _L1_xattn_in['Wo'], 'L1_ffn_gate_w': _L1_ffn_in['gate_w'], 'L1_ffn_gate_b': _L1_ffn_in['gate_b'], 'L1_ffn_expert_w': _L1_ffn_in['expert_w'], 'L1_ffn_expert_b': _L1_ffn_in['expert_b']}

def reference(x, ctx_1024, mask_Bx1x1xS2_fk0, L0_attn_Wq, L0_attn_bq, L0_attn_Wk, L0_attn_bk, L0_attn_Wv, L0_attn_bv, L0_attn_Wo, L0_attn_bo, L0_xattn_ln_g, L0_xattn_ln_b, L0_xattn_w_in, L0_xattn_wp_w1, L0_xattn_wp_b1, L0_xattn_wp_ln_g, L0_xattn_wp_ln_b, L0_xattn_wp_w2, L0_xattn_wp_b2, L0_xattn_w_out, L0_xattn_b_out, L0_ffn_gate_w, L0_ffn_expert_bias, L0_ffn_w_up, L0_ffn_w_down, L1_attn_Wq, L1_attn_bq, L1_attn_Wk, L1_attn_bk, L1_attn_Wv, L1_attn_bv, L1_attn_Wo, L1_attn_bo, L1_xattn_Wq, L1_xattn_Wk, L1_xattn_Wv, L1_xattn_Wo, L1_ffn_gate_w, L1_ffn_gate_b, L1_ffn_expert_w, L1_ffn_expert_b):
    import jax
    import jax.numpy as jnp

    def _L0_attn_ref(x, Wq, bq, Wk, bk, Wv, bv, Wo, bo):
        import jax, jax.numpy as jnp
        import numpy as np
        BASE_THETA = 0.5
        K_DOP = 0.2
        K_NOR = 0.15
        K_SERO = 0.1
        DIM = 256
        q = jnp.einsum('bsd,ed->bse', x, Wq) + bq
        k = jnp.einsum('bsd,ed->bse', x, Wk) + bk
        v = jnp.einsum('bsd,ed->bse', x, Wv) + bv
        qk = jnp.einsum('bsd,btd->bst', q, k)
        theta = BASE_THETA + K_DOP * jax.nn.sigmoid(qk) + K_NOR * jnp.tanh(qk) + K_SERO * jax.nn.relu(qk)
        attn = jax.nn.softmax(theta, axis=-1)
        out = jnp.einsum('bst,btd->bsd', attn, v)
        return jnp.einsum('bsd,ed->bse', out, Wo) + bo

    def _L0_xattn_ref(q, k, v, ln_g, ln_b, w_in, wp_w1, wp_b1, wp_ln_g, wp_ln_b, wp_w2, wp_b2, w_out, b_out):
        import jax, jax.numpy as jnp
        import numpy as np
        H, D, DIM = (8, 128, 256)
        QB, N = (16, 128)

        def layer_norm(x, g, b, eps=1e-05):
            mu = x.mean(-1, keepdims=True)
            var = ((x - mu) ** 2).mean(-1, keepdims=True)
            return (x - mu) / jnp.sqrt(var + eps) * g + b

        def proj(t):
            x = layer_norm(t, ln_g, ln_b) @ w_in.T
            Qd, Nd = (t.shape[0], t.shape[1])
            return x.reshape(Qd, Nd, H, D).transpose(2, 0, 1, 3)
        f_q, f_k, f_v = (proj(q), proj(k), proj(v))
        dots = jnp.einsum('hqnd,hqmd->hqnm', f_q, f_k)
        qn = jnp.linalg.norm(f_q, axis=-1)
        kn = jnp.linalg.norm(f_k, axis=-1)
        cosine_sim = dots / (qn[..., :, None] * kn[..., None, :])
        q_centered = f_q - f_q.mean(-1, keepdims=True)
        q_var = jnp.var(f_q, axis=-1, ddof=1)
        k_var = jnp.var(f_k, axis=-1, ddof=1)
        q_ratio = 2.0 * jnp.minimum(q_var, 1.0) / (q_var + 1.0)
        k_ratio = 2.0 * jnp.minimum(k_var, 1.0) / (k_var + 1.0)
        var_component = jnp.einsum('hqn,hqm->hqnm', q_ratio, k_ratio)
        q_flat = q_centered.reshape(H, -1, D)
        feat_corr = jnp.einsum('hnd,hne->hde', q_flat, q_flat) / q_flat.shape[1]
        feat_corr = feat_corr * (1.0 - jnp.eye(D, dtype=feat_corr.dtype))
        decorr_score = jnp.linalg.norm(feat_corr, axis=(-2, -1)) / (D * D)
        decorr_scale = jnp.exp(-5.0 * decorr_score)[:, None, None, None]
        cov_component = cosine_sim * decorr_scale
        q_global = f_q.mean(axis=(1, 2))
        k_global = f_k.mean(axis=(1, 2))
        feats = jnp.concatenate([q_global, k_global], axis=-1)
        h1 = jnp.maximum(layer_norm(feats @ wp_w1.T + wp_b1, wp_ln_g, wp_ln_b), 0.0)
        weights = jax.nn.softmax(h1 @ wp_w2.T + wp_b2, axis=-1)
        cw = weights[:, 0][:, None, None, None]
        vw = weights[:, 1][:, None, None, None]
        ww = weights[:, 2][:, None, None, None]
        mixed = cw * cosine_sim + vw * cov_component + ww * var_component
        out = jnp.einsum('hqnm,hqmd->hqnd', mixed, f_v)
        out = out.transpose(1, 2, 0, 3).reshape(q.shape[0], q.shape[1], H * D)
        return out @ w_out.T + b_out

    def _L0_ffn_ref(x, gate_w, expert_bias, w_up, w_down):
        import jax, jax.numpy as jnp
        import numpy as np
        B, S, H, E, K, I = (4, 512, 256, 8, 2, 1024)
        GATE_EPS = 1e-06
        LN_EPS = 1e-05
        logits = jnp.einsum('bsh,eh->bse', x, gate_w) + expert_bias
        weights = jax.nn.softmax(logits, axis=-1)
        top_w, top_i = jax.lax.top_k(weights, K)
        top_w = top_w / (jnp.sum(top_w, axis=-1, keepdims=True) + GATE_EPS)
        sparse_w = jnp.sum(jax.nn.one_hot(top_i, E, dtype=weights.dtype) * top_w[..., None], axis=-2)
        out = jnp.zeros_like(x)
        for e in range(E):
            h = jax.nn.gelu(jnp.einsum('bsh,ih->bsi', x, w_up[e]), approximate=False)
            y = jnp.einsum('bsi,hi->bsh', h, w_down[e])
            out = out + sparse_w[..., e:e + 1] * y
        mu = jnp.mean(out, axis=-1, keepdims=True)
        var = jnp.mean(jnp.square(out - mu), axis=-1, keepdims=True)
        out = (out - mu) * jax.lax.rsqrt(var + LN_EPS)
        return out + x

    def _L1_attn_ref(x, Wq, bq, Wk, bk, Wv, bv, Wo, bo):
        import jax, jax.numpy as jnp
        import numpy as np
        NUM_HEADS = 16
        HIDDEN = 256
        ATTN_DIM = 64
        HEAD_OUT = 64
        OUT_DIM = 256
        BATCH, SEQ = (2, 512)

        def _split_heads(y, h):
            b, s, _ = y.shape
            return y.reshape(b, s, h, -1).transpose(0, 2, 1, 3)
        h = NUM_HEADS
        q = _split_heads(x @ Wq + bq, h)
        k = _split_heads(x @ Wk + bk, h)
        v = _split_heads(x @ Wv + bv, h)
        scale = 1.0 / jnp.sqrt(jnp.float32(ATTN_DIM))
        pattern = jnp.einsum('bhid,bhjd->bhij', k, q) * scale
        prob = jax.nn.softmax(pattern, axis=-2)
        out = jnp.einsum('bhis,bhid->bhsd', prob, v)
        b, _, s, dv = out.shape
        concat = out.transpose(0, 2, 1, 3).reshape(b, s, h * dv)
        return concat @ Wo + bo

    def _L1_xattn_ref(q, k, v, mask, Wq, Wk, Wv, Wo):
        import jax, jax.numpy as jnp
        import numpy as np
        DIM, HEADS = (256, 16)
        B, S = (4, 512)
        HD = DIM // HEADS
        b, s, _ = q.shape
        qh = (q @ Wq).reshape(b, s, HEADS, HD).transpose(0, 2, 1, 3)
        kh = (k @ Wk).reshape(b, s, HEADS, HD).transpose(0, 2, 1, 3)
        vh = (v @ Wv).reshape(b, s, HEADS, HD).transpose(0, 2, 1, 3)
        g = jnp.einsum('bhqd,bhkd->bhqk', qh, kh) / jnp.sqrt(jnp.float32(HD))
        g = g - mask * 1000000000.0
        A = jax.nn.softmax(g, axis=-1)
        att = jnp.einsum('bhqk,bhkd->bhqd', A, vh)
        att = att.transpose(0, 2, 1, 3).reshape(b, s, DIM)
        return att @ Wo

    def _L1_ffn_ref(x, gate_w, gate_b, expert_w, expert_b):
        import jax, jax.numpy as jnp
        import numpy as np
        B, S, D, O, E = (8, 1024, 256, 256, 64)
        b, s, d = x.shape
        xt = x.reshape(-1, d)
        logits = xt @ gate_w.T + gate_b
        gates = jax.nn.softmax(logits, axis=-1)
        sel = jnp.argmax(gates, axis=-1)
        order = jnp.argsort(sel)
        xs = xt[order]
        counts = jnp.bincount(sel, length=E).astype(jnp.int32)
        ys = jax.lax.ragged_dot(xs, expert_w, counts)
        ys = ys + expert_b[sel[order]]
        out = jnp.zeros((xt.shape[0], expert_w.shape[-1]), dtype=ys.dtype)
        out = out.at[order].set(ys)
        return out.reshape(b, s, -1)
    x = x + _L0_attn_ref(_layernorm(x, axis=-1), L0_attn_Wq, L0_attn_bq, L0_attn_Wk, L0_attn_bk, L0_attn_Wv, L0_attn_bv, L0_attn_Wo, L0_attn_bo)
    x = x + _L0_xattn_ref(_layernorm(x, axis=-1), ctx_1024, ctx_1024, L0_xattn_ln_g, L0_xattn_ln_b, L0_xattn_w_in, L0_xattn_wp_w1, L0_xattn_wp_b1, L0_xattn_wp_ln_g, L0_xattn_wp_ln_b, L0_xattn_wp_w2, L0_xattn_wp_b2, L0_xattn_w_out, L0_xattn_b_out)
    x = x + _L0_ffn_ref(_layernorm(x, axis=-1), L0_ffn_gate_w, L0_ffn_expert_bias, L0_ffn_w_up, L0_ffn_w_down)
    x = x + _L1_attn_ref(_layernorm(x, axis=-1), L1_attn_Wq, L1_attn_bq, L1_attn_Wk, L1_attn_bk, L1_attn_Wv, L1_attn_bv, L1_attn_Wo, L1_attn_bo)
    x = x + _L1_xattn_ref(_layernorm(x, axis=-1), ctx_1024, ctx_1024, mask_Bx1x1xS2_fk0, L1_xattn_Wq, L1_xattn_Wk, L1_xattn_Wv, L1_xattn_Wo)
    x = x + _L1_ffn_ref(_layernorm(x, axis=-1), L1_ffn_gate_w, L1_ffn_gate_b, L1_ffn_expert_w, L1_ffn_expert_b)
    return x

_drawn_inputs = setup_inputs


def setup_inputs(seed=0):
    import zlib

    import numpy as np

    out = dict(_drawn_inputs(seed))
    spreads = {'L0_attn_bq': (0.0, 0.1),
     'L0_attn_bk': (0.0, 0.604),
     'L0_attn_bv': (0.0, 0.1),
     'L0_attn_bo': (0.0, 0.1),
     'L0_xattn_ln_g': (1.0, 0.2),
     'L0_xattn_ln_b': (0.0, 0.1),
     'L0_xattn_wp_b1': (0.0, 0.1),
     'L0_xattn_wp_ln_g': (1.0, 0.2),
     'L0_xattn_wp_ln_b': (0.0, 0.1),
     'L0_xattn_wp_b2': (0.0, 0.328),
     'L0_xattn_b_out': (0.0, 0.1),
     'L0_ffn_expert_bias': (0.0, 0.1),
     'L1_ffn_gate_b': (0.0, 0.1),
     'L1_ffn_expert_b': (0.0, 0.1)}
    factors = {'L1_attn_Wq': 4.812,
     'L1_attn_bq': 8.0,
     'L1_attn_Wk': 4.766,
     'L1_attn_bk': 8.0,
     'L1_attn_bv': 4.376,
     'L1_attn_bo': 4.729}
    for name, (base, spread) in spreads.items():
        noise = np.random.default_rng([zlib.crc32(name.encode()), seed]).standard_normal(out[name].shape)
        drawn = base * np.exp(spread * noise) if base else spread * noise
        out[name] = jnp.asarray(drawn.astype(out[name].dtype))
    for name, factor in factors.items():
        out[name] = (out[name] * factor).astype(out[name].dtype)
    return out
```

```python
from contextlib import ExitStack

import concourse.bass as bass
from concourse import mybir

F32 = mybir.dt.float32
I32 = mybir.dt.int32
U32 = mybir.dt.uint32
ALU = mybir.AluOpType
ACT = mybir.ActivationFunctionType
AXIS = mybir.AxisListType

P = 128
BATCH = 16
SEQ = 256
DIM = 256
TPB = SEQ // P
KC = DIM // P
TILES = BATCH * TPB
EPS = 1e-5
BUFFERS = 4


class Steps:

    def __init__(self, engine, semaphore, base=0):
        self.engine, self.semaphore, self.base, self.count = engine, semaphore, base, 0

    def counted(self, instruction):
        instruction.then_inc(self.semaphore, 1)
        self.count += 1

    def settle(self):
        self.engine.wait_ge(self.semaphore, self.base + self.count)

    def then(self, instruction):
        self.counted(instruction)
        self.settle()


def wait_past(engine, semaphore, value):
    if not isinstance(value, int) or value > 0:
        engine.wait_ge(semaphore, value)


def wait_apart(dve, semaphore, value, scratch):
    dve.wait_ge(semaphore, value)
    dve.memset(scratch, 0.0)


def pipelined(engine, front, back):
    front(0, 0)
    for b in range(2):
        front(b + 1, 1 - b)
        back(b, b)
    with engine.Fori(1, BATCH // 2 - 1) as pair:
        for p in range(2):
            front(2 * pair + (p + 1), 1 - p)
            back(2 * pair + p, p)
    front(BATCH - 1, 1)
    back(BATCH - 2, 0)
    back(BATCH - 1, 1)


class Shared:

    def __init__(self, nc, ctx):
        sb = lambda name, shape, dt=F32: ctx.enter_context(nc.sbuf_tensor(name, shape, dt))
        self.x = sb("x_resident", [P, TILES, DIM])
        self.stats = sb("x_stats", [P, TILES, 2])
        self.rstd = sb("x_rstd", [P, TILES])
        self.ident = sb("ident", [P, P])
        self.ones = sb("ones", [P, P])
        self.scratch = sb("scratch", [P, 1])
        self.sent = [ctx.enter_context(nc.semaphore(f"tokens_sent{n}")) for n in range(BUFFERS)]
        self.got = [ctx.enter_context(nc.semaphore(f"results_got{n}")) for n in range(BUFFERS)]


USED = []


def clear_semaphores(nc):
    with nc.Block() as block:

        @block.gpsimd
        def _(pool):
            for semaphore in USED:
                pool.sem_clear(semaphore)
    USED.clear()


def alloc(nc, ctx, phase):
    sb = lambda name, shape, dt=F32: ctx.enter_context(nc.sbuf_tensor(f"{phase}_{name}", shape, dt))
    ps = lambda name, shape, dt=F32: ctx.enter_context(nc.psum_tensor(f"{phase}_{name}", shape, dt))

    def sem(name):
        USED.append(ctx.enter_context(nc.semaphore(f"{phase}_{name}")))
        return USED[-1]

    return sb, ps, sem


def rows(w):
    return w.rearrange("(c p) d -> p c d", p=P)


def broadcast_row(vector, parts=P):
    return vector.rearrange("(a n) -> a n", a=1).broadcast_to([parts, vector.shape[0]])


def load_inputs(nc, sh, x, scratch=None, zeros=None, s_cleared=None):
    with ExitStack() as ctx:
        sb, ps, sem = alloc(nc, ctx, "load")
        parts = sb("parts", [P, 2, 6])
        NLOAD = 4
        s_x = [sem(f"x{n}_loaded") for n in range(NLOAD)]
        s_zero, s_const, s_dve, s_zeros = sem("zeroed"), sem("const"), sem("dve_step"), sem("zeros_ready")
        per = TILES // NLOAD
        xt = x.rearrange("b (t p) d -> p (b t) d", p=P)
        with nc.Block() as block:

            @block.sync
            def _(sp):
                for n in range(NLOAD):
                    sp.dma_start(sh.x[:, n * per:(n + 1) * per, :], xt[:, n * per:(n + 1) * per, :]).then_inc(s_x[n], 16)
                if scratch:
                    sp.wait_ge(s_zeros, 1)
                    for n in range(CLEARS):
                        dst = scratch.tokens[n * CLEAR_ROWS:(n + 1) * CLEAR_ROWS, :].rearrange("(p r) d -> p (r d)", p=P)
                        sp.dma_start(dst, zeros[:]).then_inc(s_cleared, 16)

            @block.gpsimd
            def _(pool):
                if scratch:
                    pool.memset(zeros[:], 0.0).then_inc(s_zeros, 1)
                pool.memset(sh.ident[:], 0.0).then_inc(s_zero, 1)
                pool.memset(sh.ones[:], 1.0).then_inc(s_const, 1)
                pool.wait_ge(s_zero, 1)
                pool.affine_select(out=sh.ident[:], in_=sh.ident[:], compare_op=ALU.not_equal, fill=1.0, base=0,
                                   pattern=[[-1, P]], channel_multiplier=1).then_inc(s_const, 1)
                pool.wait_ge(s_const, 2)

            @block.vector
            def _(dve):
                step = Steps(dve, s_dve)
                for t in range(TILES):
                    if t % per == 0:
                        dve.wait_ge(s_x[t // per], 16)
                    token_stats(dve, step, sh, t, parts[:, t % 2, :])


MAX_TILES = 96
ROWS = MAX_TILES * P
CLEAR_ROWS = P * 8
CLEARS = ROWS // CLEAR_ROWS


class Sorted:

    def __init__(self, nc):
        self.tokens = nc.dram_tensor("sorted_tokens", [ROWS, DIM], F32, kind="Internal").ap()
        self.results = nc.dram_tensor("sorted_results", [ROWS, DIM], F32, kind="Internal").ap()


def token_stats(dve, step, sh, tile, parts):
    step.then(dve.bn_stats(parts, sh.x[:, tile, :]))
    step.counted(dve.bn_aggr(sh.stats[:, tile, :], parts))


def batch_stats(dve, step, sh, batch, parts, means):
    for t in range(TPB):
        instruction = dve.bn_stats(parts[:, t, :], sh.x[:, TPB * batch + t, :])
    step.counted(instruction)
    wait_apart(dve, step.semaphore, step.base + step.count, sh.scratch[:])
    for t in range(TPB):
        instruction = dve.bn_aggr(means[:, t, :], parts[:, t, :])
    step.counted(instruction)
    dve.wait_ge(step.semaphore, step.base + step.count)
    step.counted(dve.tensor_scalar(sh.stats[:, bass.ds(TPB * batch, TPB), :], means, 1.0, None, ALU.mult))


STATS_STEPS = 3


def norm_scales(nc, sh, name, twice=False):
    with ExitStack() as ctx:
        sb, ps, sem = alloc(nc, ctx, name)
        var = sb("var", [P, TILES])
        std = sb("std", [P, TILES])
        first = sb("first", [P, TILES])
        s_dve, s_std = sem("dve_step"), sem("std_ready")
        with nc.Block() as block:

            @block.vector
            def _(dve):
                step = Steps(dve, s_dve)
                step.then(dve.tensor_scalar(var[:], sh.stats[:, :, 1], EPS, None, ALU.add))
                dve.wait_ge(s_std, 1)
                if not twice:
                    step.then(dve.reciprocal(sh.rstd[:], std[:]))
                    return
                step.then(dve.reciprocal(first[:], std[:]))
                step.then(dve.tensor_tensor(var[:], first[:], first[:], ALU.mult))
                step.then(dve.tensor_tensor(var[:], var[:], sh.stats[:, :, 1], ALU.mult))
                step.then(dve.tensor_scalar(var[:], var[:], EPS, None, ALU.add))
                dve.wait_ge(s_std, 2)
                step.then(dve.reciprocal(std[:], std[:]))
                step.then(dve.tensor_tensor(sh.rstd[:], first[:], std[:], ALU.mult))

            @block.scalar
            def _(act):
                act.wait_ge(s_dve, 1)
                act.activation(std[:], var[:], ACT.Sqrt).then_inc(s_std, 1)
                if twice:
                    act.wait_ge(s_dve, 5)
                    act.activation(std[:], var[:], ACT.Sqrt).then_inc(s_std, 1)


def l0_attention(nc, sh, Wq, bq, Wk, bk, Wv, bv, Wo, bo, s_cleared=None):
    with ExitStack() as ctx:
        sb, ps, sem = alloc(nc, ctx, "a0")
        w_nat = sb("w_nat", [P, 4, KC, DIM])
        b_col = sb("b_col", [P, 3, KC])
        woT = sb("woT", [P, KC, DIM])
        mqk = sb("mqk", [P, KC, DIM])
        wvoT = sb("wvoT", [P, KC, DIM])
        ucol = sb("ucol", [P, KC])
        qbias = sb("qbias", [P, KC])
        bq_wide = sb("bq_wide", [P, KC, P])
        bv_wide = sb("bv_wide", [P, KC, P])
        cq = sb("cq", [P, 1])
        vbias = sb("vbias", [P, DIM])
        wt = ps("wt", [P, 512])
        s_w, s_b = sem("weights_loaded"), sem("biases_loaded")
        s_pe, s_sb, s_wide = sem("prep_in_psum"), sem("prep_in_sbuf"), sem("wide")
        with nc.Block() as block:

            @block.sync
            def _(sp):
                for n, w in enumerate((Wq, Wk, Wv, Wo)):
                    sp.dma_start(w_nat[:, n], rows(w)).then_inc(s_w, 16)
                sp.dma_start(vbias[:], broadcast_row(bo)).then_inc(s_b, 16)

            @block.scalar
            def _(act):
                for n, b in enumerate((bq, bk, bv)):
                    for k in range(KC):
                        act.dma_start(b_col[:, n, k:k + 1], b[k * P:(k + 1) * P].rearrange("(p a) -> p a", a=1)).then_inc(s_b, 16)

            @block.tensor
            def _(pe):
                pe.wait_ge(s_w, 64)
                for k in range(KC):
                    for m in range(KC):
                        last = pe.transpose(wt[:, (k * KC + m) * P:(k * KC + m + 1) * P], w_nat[:, 3, m, k * P:(k + 1) * P],
                                            sh.ident[:])
                last.then_inc(s_pe, 1)
                pe.wait_ge(s_sb, 1)
                for m in range(KC):
                    for k in range(KC):
                        last = pe.matmul(wt[:, m * DIM:(m + 1) * DIM], w_nat[:, 0, k, m * P:(m + 1) * P], w_nat[:, 1, k, :],
                                         start=k == 0, stop=k == KC - 1)
                last.then_inc(s_pe, 1)
                pe.wait_ge(s_sb, 2)
                for m in range(KC):
                    for k in range(KC):
                        last = pe.matmul(wt[:, m * DIM:(m + 1) * DIM], w_nat[:, 2, k, m * P:(m + 1) * P], woT[:, k, :],
                                         start=k == 0, stop=k == KC - 1)
                last.then_inc(s_pe, 1)
                pe.wait_ge(s_sb, 3)
                pe.wait_ge(s_b, 16 * 7)
                for m in range(KC):
                    for k in range(KC):
                        pe.matmul(wt[:, m:m + 1], w_nat[:, 0, k, m * P:(m + 1) * P], b_col[:, 1, k:k + 1],
                                  start=k == 0, stop=k == KC - 1)
                    for k in range(KC):
                        pe.matmul(wt[:, 2 + m:3 + m], w_nat[:, 1, k, m * P:(m + 1) * P], b_col[:, 0, k:k + 1],
                                  start=k == 0, stop=k == KC - 1)
                pe.wait_ge(s_wide, 2 * KC)
                for k in range(KC):
                    pe.matmul(wt[:, 4:5], bq_wide[:, k, :], b_col[:, 1, k:k + 1], start=k == 0, stop=k == KC - 1)
                for k in range(KC):
                    last = pe.matmul(wt[:, 256:512], bv_wide[:, k, :], woT[:, k, :], start=k == 0, stop=k == KC - 1)
                last.then_inc(s_pe, 1)

            @block.vector
            def _(dve):
                dve.wait_ge(s_b, 16 * 7)
                for k in range(KC):
                    dve.tensor_scalar(bq_wide[:, k, :], sh.ones[:], b_col[:, 0, k:k + 1], None, ALU.mult).then_inc(s_wide, 1)
                    dve.tensor_scalar(bv_wide[:, k, :], sh.ones[:], b_col[:, 2, k:k + 1], None, ALU.mult).then_inc(s_wide, 1)
                for n, out in enumerate((woT, mqk, wvoT)):
                    dve.wait_ge(s_pe, n + 1)
                    dve.tensor_copy(out[:].rearrange("p k d -> p (k d)"), wt[:]).then_inc(s_sb, 1)
                dve.wait_ge(s_pe, 4)
                dve.tensor_copy(ucol[:], wt[:, 0:2]).then_inc(s_sb, 1)
                dve.tensor_copy(qbias[:], wt[:, 2:4]).then_inc(s_sb, 1)
                dve.tensor_copy(cq[:], wt[:, 4:5]).then_inc(s_sb, 1)
                dve.tensor_tensor(vbias[:], wt[:, 256:512], vbias[:], ALU.add).then_inc(s_sb, 1)
                dve.wait_ge(s_sb, 7)

        xn = sb("xn", [P, 2, TPB, DIM])
        xT = sb("xT", [P, 2, KC, SEQ])
        qT = sb("qT", [P, 2, KC, SEQ])
        v = sb("v", [P, 2, TPB, DIM])
        srow = sb("srow", [P, 2, TPB])
        shalf = sb("shalf", [P, 2, TPB])
        t1 = sb("t1", [P, 2, TPB, SEQ])
        t2 = sb("t2", [P, 2, TPB, SEQ])
        th = sb("th", [P, 2, TPB, SEQ])
        top = sb("top", [P, 2, TPB])
        prob = sb("prob", [P, 2, TPB, SEQ])
        den = sb("den", [P, 2, TPB])
        rden = sb("rden", [P, 2, TPB])
        pT = sb("pT", [P, 2, TPB, SEQ])
        parts = sb("parts", [P, TPB, 6])
        means = sb("means", [P, TPB, 2])
        q_ps = ps("q_ps", [P, KC, SEQ])
        v_ps = ps("v_ps", [P, TPB, DIM])
        s_ps = [ps(f"s_ps{n}", [P, TPB, SEQ]) for n in range(2)]
        pT_ps = ps("pT_ps", [P, TPB, SEQ])
        o_ps = ps("o_ps", [P, TPB, DIM])
        c_ps = ps("c_ps", [P, 2, TPB])
        xT_ps = wt
        s_xn, s_xTp, s_xT = sem("xn_ready"), sem("xT_in_psum"), sem("xT_ready")
        s_qp, s_q, s_vp, s_v, s_row = sem("q_in_psum"), sem("q_ready"), sem("v_in_psum"), sem("v_ready"), sem("row_bias_ready")
        s_sc, s_tanh, s_relu, s_top = sem("scores_in_psum"), sem("tanhs_ready"), sem("relu_ready"), sem("top_ready")
        s_prob, s_pTp, s_pT, s_op, s_x = (sem("probs_ready"), sem("pT_in_psum"), sem("pT_ready"), sem("out_in_psum"),
                                         sem("x_updated"))
        s_front, s_back = sem("front_step"), sem("back_step")
        FRONT, BACK = 4, 1 + STATS_STEPS

        with nc.Block() as block:
            if s_cleared:

                @block.sync
                def _(sp):
                    sp.wait_ge(s_cleared, 16 * CLEARS)

            @block.tensor
            def _(pe):
                def front(b, p):
                    pe.wait_ge(s_xn, b + 1)
                    wait_past(pe, s_xT, b)
                    for k in range(KC):
                        for t in range(TPB):
                            last = pe.transpose(xT_ps[:, k * SEQ + t * P:k * SEQ + (t + 1) * P], xn[:, p, t, k * P:(k + 1) * P],
                                                sh.ident[:])
                    last.then_inc(s_xTp, 1)
                    pe.wait_ge(s_xT, b + 1)
                    wait_past(pe, s_q, b)
                    for m in range(KC):
                        for k in range(KC):
                            last = pe.matmul(q_ps[:, m, :], mqk[:, k, m * P:(m + 1) * P], xT[:, p, k, :], start=k == 0,
                                             stop=k == KC - 1)
                    last.then_inc(s_qp, 1)
                    wait_past(pe, s_v, b)
                    for t in range(TPB):
                        for k in range(KC):
                            pe.matmul(v_ps[:, t, :], xT[:, p, k, t * P:(t + 1) * P], wvoT[:, k, :], start=k == 0,
                                      stop=k == KC - 1)
                    for t in range(TPB):
                        for k in range(KC):
                            last = pe.matmul(c_ps[:, p, t:t + 1], xT[:, p, k, t * P:(t + 1) * P], ucol[:, k:k + 1],
                                             start=k == 0, stop=k == KC - 1)
                    last.then_inc(s_vp, 1)
                    pe.wait_ge(s_q, b + 1)
                    wait_past(pe, s_tanh, b - 1)
                    wait_past(pe, s_relu, b - 1)
                    for t in range(TPB):
                        for k in range(KC):
                            last = pe.matmul(s_ps[p][:, t, :], qT[:, p, k, t * P:(t + 1) * P], xT[:, p, k, :], start=k == 0,
                                             stop=k == KC - 1)
                    last.then_inc(s_sc, 1)

                def back(b, p):
                    pe.wait_ge(s_prob, b + 1)
                    wait_past(pe, s_pT, b)
                    for j in range(TPB):
                        for t in range(TPB):
                            last = pe.transpose(pT_ps[:, j, t * P:(t + 1) * P], prob[:, p, t, j * P:(j + 1) * P], sh.ident[:])
                    last.then_inc(s_pTp, 1)
                    pe.wait_ge(s_pT, b + 1)
                    pe.wait_ge(s_v, b + 1)
                    wait_past(pe, s_x, TPB * b)
                    for t in range(TPB):
                        for j in range(TPB):
                            last = pe.matmul(o_ps[:, t, :], pT[:, p, j, t * P:(t + 1) * P], v[:, p, j, :], start=j == 0,
                                             stop=j == TPB - 1)
                    last.then_inc(s_op, 1)

                pipelined(pe, front, back)

            @block.scalar
            def _(act):
                def front(b, p):
                    act.wait_ge(s_xTp, b + 1)
                    act.copy(xT[:, p].rearrange("p k s -> p (k s)"), xT_ps[:]).then_inc(s_xT, 1)
                    act.wait_ge(s_qp, b + 1)
                    act.activation(qT[:, p, 0, :], q_ps[:, 0, :], ACT.Identity, bias=qbias[:, 0:1])
                    act.activation(qT[:, p, 1, :], q_ps[:, 1, :], ACT.Identity, bias=qbias[:, 1:2]).then_inc(s_q, 1)
                    act.wait_ge(s_sc, b + 1)
                    act.wait_ge(s_row, b + 1)
                    for t in range(TPB):
                        act.activation(t1[:, p, t, :], s_ps[p][:, t, :], ACT.Tanh, bias=shalf[:, p, t:t + 1], scale=0.5)
                        last = act.activation(t2[:, p, t, :], s_ps[p][:, t, :], ACT.Tanh, bias=srow[:, p, t:t + 1])
                    last.then_inc(s_tanh, 1)

                def back(b, p):
                    act.wait_ge(s_top, b + 1)
                    for t in range(TPB):
                        last = act.activation(prob[:, p, t, :], th[:, p, t, :], ACT.Exp, bias=top[:, p, t:t + 1], scale=0.1,
                                              accum_out=den[:, p, t:t + 1])
                    last.then_inc(s_prob, 1)
                    act.wait_ge(s_pTp, b + 1)
                    act.copy(pT[:, p].rearrange("p j s -> p (j s)"), pT_ps[:].rearrange("p j s -> p (j s)")).then_inc(s_pT, 1)

                pipelined(act, front, back)

            @block.vector
            def _(dve):
                def normalise(b, p):
                    for t in range(TPB):
                        last = dve.tensor_scalar(xn[:, p, t, :], sh.x[:, TPB * b + t, :], sh.stats[:, TPB * b + t, 0:1],
                                                 sh.rstd[:, bass.ds(TPB * b + t, 1)], ALU.subtract, ALU.mult)
                        last.then_inc(s_xn, 1) if t == TPB - 1 else None

                def front(b, p):
                    normalise(b, p)
                    step = Steps(dve, s_front, b * FRONT)
                    dve.wait_ge(s_vp, b + 1)
                    step.then(dve.tensor_scalar(srow[:, p, :], c_ps[:, p, :], cq[:, 0:1], None, ALU.add))
                    dve.tensor_scalar(shalf[:, p, :], srow[:, p, :], 0.5, None, ALU.mult).then_inc(s_row, 1)
                    for t in range(TPB):
                        last = dve.tensor_tensor(v[:, p, t, :], v_ps[:, t, :], vbias[:], ALU.add)
                    last.then_inc(s_v, 1)
                    dve.wait_ge(s_tanh, b + 1)
                    for t in range(TPB):
                        last = dve.tensor_scalar(th[:, p, t, :], s_ps[p][:, t, :], srow[:, p, t:t + 1], 0.0, ALU.add, ALU.max)
                    last.then_inc(s_relu, 1)
                    step.then(dve.scalar_tensor_tensor(t1[:, p], t2[:, p], 1.5, t1[:, p], ALU.mult, ALU.add))
                    step.then(dve.tensor_tensor(th[:, p], th[:, p], t1[:, p], ALU.add))
                    step.then(dve.tensor_reduce(top[:, p], th[:, p], AXIS.X, ALU.max))
                    dve.tensor_scalar(top[:, p], top[:, p], -0.1, None, ALU.mult).then_inc(s_top, 1)
                    assert step.count == FRONT

                def back(b, p):
                    step = Steps(dve, s_back, b * BACK)
                    dve.wait_ge(s_prob, b + 1)
                    step.then(dve.reciprocal(rden[:, p], den[:, p]))
                    dve.wait_ge(s_op, b + 1)
                    for t in range(TPB):
                        last = dve.scalar_tensor_tensor(sh.x[:, TPB * b + t, :], o_ps[:, t, :], rden[:, p, t:t + 1],
                                                        sh.x[:, TPB * b + t, :], ALU.mult, ALU.add)
                        last.then_inc(s_x, 1)
                    wait_apart(dve, s_x, TPB * (b + 1), sh.scratch[:])
                    batch_stats(dve, step, sh, b, parts, means[:])
                    assert step.count == BACK

                pipelined(dve, front, back)


XH = 8
HD = 128
INNER = XH * HD


def l0_cross_attention(nc, sh, ctx_in, ln_g, ln_b, w_in, w1, b1, g1, be1, w2, b2, w_out, b_out):
    with ExitStack() as ctx:
        sb, ps, sem = alloc(nc, ctx, "x0")
        context = sb("context", [P, TILES, DIM])
        c_stats = sb("c_stats", [P, TILES, 2])
        c_rstd = sb("c_rstd", [P, TILES])
        wgT = sb("wgT", [P, KC, INNER])
        woT = sb("woT", [P, XH, DIM])
        fbias = sb("fbias", [P, INNER])
        out_bias = sb("out_bias", [P, DIM])
        c1 = sb("c1", [P, XH])
        ww = sb("ww", [XH, 1])
        bank = [ps(f"bank{n}", [P, 512]) for n in range(8)]

        l0_cross_weights(nc, sh, bank, ctx_in, ln_g, ln_b, w_in, w_out, b_out, context, c_stats, c_rstd, wgT, woT, fbias,
                         out_bias)
        l0_cross_mixing(nc, sh, bank, context, c_stats, c_rstd, wgT, fbias, w1, b1, g1, be1, w2, b2, c1, ww)
        l0_cross_batches(nc, sh, bank, context, c_stats, c_rstd, wgT, woT, fbias, out_bias, c1, ww)


def l0_cross_weights(nc, sh, bank, ctx_in, ln_g, ln_b, w_in, w_out, b_out, context, c_stats, c_rstd, wgT, woT, fbias,
                     out_bias):
    with ExitStack() as ctx:
        sb, ps, sem = alloc(nc, ctx, "x0w")
        w_nat = sb("w_nat", [P, XH, DIM])
        wo_nat = sb("wo_nat", [P, KC, INNER])
        g_col = sb("g_col", [P, KC])
        b_col = sb("b_col", [P, KC])
        b_wide = sb("b_wide", [P, KC, P])
        parts = sb("parts", [P, 2, 6])
        std = sb("std", [P, TILES])
        NLOAD = 4
        per = TILES // NLOAD
        s_c = [sem(f"context{n}_loaded") for n in range(NLOAD)]
        s_w, s_col = sem("weights_loaded"), sem("columns_loaded")
        s_ps, s_sb, s_wide = sem("turned_in_psum"), sem("turned_in_sbuf"), sem("wide")
        s_dve, s_std = sem("dve_step"), sem("std_ready")
        with nc.Block() as block:

            @block.sync
            def _(sp):
                sp.dma_start(w_nat[:], rows(w_in)).then_inc(s_w, 16)
                sp.dma_start(wo_nat[:], rows(w_out)).then_inc(s_w, 16)
                sp.dma_start(out_bias[:], broadcast_row(b_out)).then_inc(s_w, 16)
                tokens = ctx_in.rearrange("b (t p) d -> p (b t) d", p=P)
                for n in range(NLOAD):
                    sp.dma_start(context[:, n * per:(n + 1) * per, :], tokens[:, n * per:(n + 1) * per, :]).then_inc(s_c[n], 16)

            @block.scalar
            def _(act):
                with nc.allow_non_contiguous_dma("columns of the normalisation"):
                    act.dma_start(g_col[:], ln_g.rearrange("(c p) -> p c", p=P)).then_inc(s_col, 16)
                    act.dma_start(b_col[:], ln_b.rearrange("(c p) -> p c", p=P)).then_inc(s_col, 16)
                act.wait_ge(s_dve, 2 * TILES + 1)
                act.activation(std[:], std[:], ACT.Sqrt).then_inc(s_std, 1)

            @block.tensor
            def _(pe):
                pe.wait_ge(s_w, 48)
                for k in range(KC):
                    for h in range(XH):
                        last = pe.transpose(bank[2 * k + h // 4][:, h % 4 * P:(h % 4 + 1) * P], w_nat[:, h, k * P:(k + 1) * P],
                                            sh.ident[:])
                    last.then_inc(s_ps, 1)
                for h in range(XH):
                    for m in range(KC):
                        last = pe.transpose(bank[4 + h // 2][:, h % 2 * DIM + m * P:h % 2 * DIM + (m + 1) * P],
                                            wo_nat[:, m, h * P:(h + 1) * P], sh.ident[:])
                last.then_inc(s_ps, 1)
                pe.wait_ge(s_sb, 2 * KC)
                pe.wait_ge(s_wide, KC)
                for half in range(2):
                    for k in range(KC):
                        last = pe.matmul(bank[half][:], b_wide[:, k, :], wgT[:, k, half * 512:(half + 1) * 512], start=k == 0,
                                         stop=k == KC - 1)
                last.then_inc(s_ps, 1)

            @block.vector
            def _(dve):
                dve.wait_ge(s_col, 32)
                for k in range(KC):
                    dve.tensor_scalar(b_wide[:, k, :], sh.ones[:], b_col[:, k:k + 1], None, ALU.mult).then_inc(s_wide, 1)
                for k in range(KC):
                    dve.wait_ge(s_ps, k + 1)
                    for half in range(2):
                        dve.tensor_copy(wgT[:, k, half * 512:(half + 1) * 512], bank[2 * k + half][:]).then_inc(s_sb, 1)
                dve.wait_ge(s_ps, KC + 1)
                for n in range(4):
                    dve.tensor_copy(woT[:, 2 * n:2 * n + 2, :].rearrange("p h d -> p (h d)"), bank[4 + n][:])
                dve.wait_ge(s_ps, KC + 2)
                for half in range(2):
                    dve.tensor_copy(fbias[:, half * 512:(half + 1) * 512], bank[half][:])
                for k in range(KC):
                    dve.tensor_scalar(wgT[:, k, :], wgT[:, k, :], g_col[:, k:k + 1], None, ALU.mult)
                step = Steps(dve, s_dve)
                for t in range(TILES):
                    if t % per == 0:
                        dve.wait_ge(s_c[t // per], 16)
                    step.then(dve.bn_stats(parts[:, t % 2, :], context[:, t, :]))
                    step.counted(dve.bn_aggr(c_stats[:, t, :], parts[:, t % 2, :]))
                step.settle()
                step.then(dve.tensor_scalar(std[:], c_stats[:, :, 1], EPS, None, ALU.add))
                dve.wait_ge(s_std, 1)
                step.then(dve.reciprocal(c_rstd[:], std[:]))



def l0_cross_mixing(nc, sh, bank, context, c_stats, c_rstd, wgT, fbias, w1, b1, g1, be1, w2, b2, c1, ww):
    TOKENS = BATCH * SEQ
    with ExitStack() as ctx:
        sb, ps, sem = alloc(nc, ctx, "x0m")
        xn = sb("xn", [P, 2, TPB, DIM + 2])
        cn = sb("cn", [P, 2, TPB, DIM])
        gram = sb("gram", [P, KC, DIM])
        sums = sb("sums", [P, KC, 2])
        means = sb("means", [P, KC, 2])
        wcT = sb("wcT", [P, KC, INNER])
        wmean = sb("wmean", [P, KC, XH])
        bmean = sb("bmean", [1, XH])
        bc = sb("bc", [1, INNER])
        prow = sb("prow", [1, INNER])
        rrow = sb("rrow", [1, INNER])
        y = sb("y", [P, KC, INNER])
        offdiag = sb("offdiag", [P, P])
        corr = sb("corr", [P, XH, P])
        sq = sb("sq", [P, XH, P])
        fsq = sb("fsq", [P, XH])
        decorr = sb("decorr", [P, XH])
        feats = sb("feats", [P, 2, XH])
        w1_nat = sb("w1_nat", [P, 2 * P])
        w1T = sb("w1T", [P, 2, P])
        w2T = sb("w2T", [P, 3])
        rows8 = sb("rows8", [XH, 3, P])
        b2_8 = sb("b2_8", [XH, 3])
        h1 = sb("h1", [XH, P])
        hparts = sb("hparts", [XH, 6])
        hstat = sb("hstat", [XH, 2])
        hstd = sb("hstd", [XH, 1])
        h1T = sb("h1T", [P, XH])
        logits = sb("logits", [XH, 3])
        lmax = sb("lmax", [XH, 1])
        expo = sb("expo", [XH, 3])
        esum = sb("esum", [XH, 1])
        wts = sb("wts", [XH, 3])
        diag = sb("diag", [XH, 2, XH])
        s_load, s_col = sem("loaded"), sem("w2_loaded")
        s_n, s_acc, s_ps, s_act, s_dve, s_one = (sem("normalised"), sem("batch_summed"), sem("in_psum"), sem("act_step"),
                                                 sem("dve_step"), sem("ones_ready"))

        with nc.Block() as block:

            @block.sync
            def _(sp):
                sp.dma_start(w1_nat[:], w1).then_inc(s_load, 16)
                for n, r in enumerate((b1, g1, be1)):
                    sp.dma_start(rows8[:, n, :], broadcast_row(r, XH)).then_inc(s_load, 16)
                sp.dma_start(b2_8[:], broadcast_row(b2, XH)).then_inc(s_load, 16)
                with nc.allow_non_contiguous_dma("384 words"):
                    sp.dma_start(w2T[:], w2.rearrange("c p -> p c")).then_inc(s_col, 16)


            def over_batches(engine, batch):
                batch(0, 0)
                batch(1, 1)
                with engine.Fori(1, BATCH // 2 - 1) as pair:
                    for p in range(2):
                        batch(2 * pair + p, p)
                batch(BATCH - 2, 0)
                batch(BATCH - 1, 1)

            G_SB, WC, ROWS, Y_SB, CORR, FEATS, H1, HVAR, H1N, H1T, LMAX, WTS, DIAG = range(1, 14)

            @block.tensor
            def _(pe):
                def batch(b, p):
                    pe.wait_ge(s_n, b + 1)
                    first, last = isinstance(b, int) and b == 0, isinstance(b, int) and b == BATCH - 1
                    for t in range(TPB):
                        a, z = first and t == 0, last and t == TPB - 1
                        for m in range(KC):
                            pe.matmul(bank[m][:, 0:DIM + 2], xn[:, p, t, m * P:(m + 1) * P], xn[:, p, t, :], start=a, stop=z)
                        for m in range(KC):
                            ins = pe.matmul(bank[2 + m][:, 0:1], cn[:, p, t, m * P:(m + 1) * P], sh.ones[:, 0:1], start=a,
                                            stop=z)
                    ins.then_inc(s_acc, 1)

                over_batches(pe, batch)
                pe.wait_ge(s_dve, WC)
                for m in range(KC):
                    for half in range(2):
                        for k in range(KC):
                            pe.matmul(bank[2 * m + half][:], gram[:, k, m * P:(m + 1) * P],
                                      wcT[:, k, half * 512:(half + 1) * 512], start=k == 0, stop=k == KC - 1)
                for half in range(2):
                    for k in range(KC):
                        last = pe.matmul(bank[4 + half][0:1, :], sums[:, k, 0:1], wcT[:, k, half * 512:(half + 1) * 512],
                                         start=k == 0, stop=k == KC - 1)
                last.then_inc(s_ps, 1)
                pe.wait_ge(s_dve, Y_SB)
                for h in range(XH):
                    o = bank[h // 4][:, h % 4 * P:(h % 4 + 1) * P]
                    cols = slice(h * P, (h + 1) * P)
                    for k in range(KC):
                        pe.matmul(o, wcT[:, k, cols], y[:, k, cols], start=k == 0, stop=False)
                    pe.matmul(o, prow[0:1, cols], bc[0:1, cols], start=False, stop=False)
                    last = pe.matmul(o, bc[0:1, cols], rrow[0:1, cols], start=False, stop=True)
                for h in range(XH):
                    o = bank[2][:, 2 * h:2 * h + 2]
                    for k in range(KC):
                        pe.matmul(o, wgT[:, k, h * P:(h + 1) * P], means[:, k, :], start=k == 0, stop=False)
                    last = pe.matmul(o, fbias[0:1, h * P:(h + 1) * P], sh.ones[0:1, 0:2], start=False, stop=True)
                pe.wait_ge(s_load, 80)
                for j in range(2):
                    last = pe.transpose(bank[3][:, j * P:(j + 1) * P], w1_nat[:, j * P:(j + 1) * P], sh.ident[:])
                last.then_inc(s_ps, 1)
                pe.wait_ge(s_dve, FEATS)
                for j in range(2):
                    last = pe.matmul(bank[4][0:XH, 0:P], feats[:, j, :], w1T[:, j, :], start=j == 0, stop=j == 1)
                last.then_inc(s_ps, 1)
                pe.wait_ge(s_act, 2)
                pe.matmul(bank[5][:, 0:XH], sh.ones[:], fsq[:], start=True, stop=True).then_inc(s_ps, 1)
                pe.wait_ge(s_dve, H1N)
                pe.transpose(bank[6][:, 0:XH], h1[:], sh.ident[0:XH, 0:XH]).then_inc(s_ps, 1)
                pe.wait_ge(s_dve, H1T)
                pe.wait_ge(s_col, 16)
                pe.matmul(bank[7][0:XH, 0:3], h1T[:], w2T[:], start=True, stop=True).then_inc(s_ps, 1)
                pe.wait_ge(s_dve, DIAG)
                pe.matmul(bank[4][:, 0:2 * XH], sh.ones[0:XH, :], diag[:].rearrange("p a h -> p (a h)"), start=True,
                          stop=True).then_inc(s_ps, 1)

            @block.scalar
            def _(act):
                act.wait_ge(s_dve, CORR)
                for h in range(XH):
                    last = act.activation(sq[:, h, :], corr[:, h, :], ACT.Square, accum_out=fsq[:, h:h + 1])
                    if h == 0:
                        last.then_inc(s_act, 1)
                last.then_inc(s_act, 1)
                act.wait_ge(s_dve, HVAR)
                act.activation(hstd[:], hstd[:], ACT.Sqrt).then_inc(s_act, 1)
                act.wait_ge(s_ps, 4)
                act.activation(decorr[:], bank[5][:, 0:XH], ACT.Sqrt).then_inc(s_act, 1)
                act.wait_ge(s_act, 4)
                act.activation(decorr[:], decorr[:], ACT.Exp, scale=-5.0 / (HD * HD)).then_inc(s_act, 1)
                act.wait_ge(s_dve, LMAX)
                act.activation(expo[:], logits[:], ACT.Exp, bias=lmax[:], accum_out=esum[:]).then_inc(s_act, 1)

            s_own = sem("own_step")

            @block.vector
            def _(dve):
                for p in range(2):
                    dve.memset(xn[:, p, :, DIM:DIM + 2], 1.0).then_inc(s_one, 1)

                def batch(b, p):
                    wait_past(dve, s_acc, b - 1)
                    for t in range(TPB):
                        tile = TPB * b + t
                        dve.tensor_scalar(xn[:, p, t, 0:DIM], sh.x[:, tile, :], sh.stats[:, tile, 0:1],
                                          sh.rstd[:, bass.ds(tile, 1)], ALU.subtract, ALU.mult)
                        ins = dve.tensor_scalar(cn[:, p, t, :], context[:, tile, :], c_stats[:, tile, 0:1],
                                                c_rstd[:, bass.ds(tile, 1)], ALU.subtract, ALU.mult)
                    ins.then_inc(s_n, 1)

                over_batches(dve, batch)
                step = Steps(dve, s_own)
                dve.wait_ge(s_acc, BATCH)
                for m in range(KC):
                    dve.tensor_copy(gram[:, m, :], bank[m][:, 0:DIM])
                    dve.tensor_copy(sums[:, m, 0:1], bank[m][:, DIM:DIM + 1])
                    last = dve.tensor_copy(sums[:, m, 1:2], bank[2 + m][:, 0:1])
                step.then(last)
                dve.tensor_scalar(means[:], sums[:], 1.0 / TOKENS, None, ALU.mult).then_inc(s_dve, 1)
                for k in range(KC):
                    last = dve.tensor_reduce(wmean[:, k, :], wgT[:, k, :].rearrange("p (h d) -> p h d", d=HD), AXIS.X, ALU.add)
                step.then(last)
                step.then(dve.tensor_scalar(wmean[:], wmean[:], 1.0 / HD, None, ALU.mult))
                for k in range(KC):
                    last = dve.tensor_tensor(wcT[:, k, :].rearrange("p (h d) -> p h d", d=HD),
                                             wgT[:, k, :].rearrange("p (h d) -> p h d", d=HD),
                                             wmean[:, k, :].unsqueeze(2).broadcast_to([P, XH, HD]), ALU.subtract)
                last.then_inc(s_dve, 1)
                step.then(dve.tensor_reduce(bmean[:], fbias[0:1, :].rearrange("p (h d) -> p h d", d=HD), AXIS.X, ALU.add))
                step.then(dve.tensor_scalar(bmean[:], bmean[:], 1.0 / HD, None, ALU.mult))
                step.then(dve.tensor_tensor(bc[:].rearrange("p (h d) -> p h d", d=HD),
                                            fbias[0:1, :].rearrange("p (h d) -> p h d", d=HD),
                                            bmean[:].unsqueeze(2).broadcast_to([1, XH, HD]), ALU.subtract))
                dve.wait_ge(s_ps, 1)
                for half in range(2):
                    last = dve.tensor_copy(prow[0:1, half * 512:(half + 1) * 512], bank[4 + half][0:1, :])
                step.then(last)
                dve.scalar_tensor_tensor(rrow[:], bc[:], float(TOKENS), prow[:], ALU.mult, ALU.add).then_inc(s_dve, 1)
                for m in range(KC):
                    for half in range(2):
                        last = dve.tensor_copy(y[:, m, half * 512:(half + 1) * 512], bank[2 * m + half][:])
                last.then_inc(s_dve, 1)
                step.then(dve.tensor_scalar(offdiag[:], sh.ident[:], -1.0 / TOKENS, 1.0 / TOKENS, ALU.mult, ALU.add))
                dve.wait_ge(s_ps, 2)
                for half in range(2):
                    last = dve.tensor_tensor(corr[:, 4 * half:4 * half + 4, :], bank[half][:].rearrange("p (h d) -> p h d", d=P),
                                             offdiag[:].unsqueeze(1).broadcast_to([P, 4, P]), ALU.mult)
                last.then_inc(s_dve, 1)
                dve.tensor_copy(w1T[:].rearrange("p j d -> p (j d)"), bank[3][:, 0:2 * P])
                dve.tensor_copy(feats[:], bank[2][:, 0:2 * XH].rearrange("p (h a) -> p a h", a=2)).then_inc(s_dve, 1)
                dve.wait_ge(s_ps, 3)
                dve.tensor_tensor(h1[:], bank[4][0:XH, 0:P], rows8[:, 0, :], ALU.add).then_inc(s_dve, 1)
                dve.wait_ge(s_dve, H1)
                step.then(dve.bn_stats(hparts[:], h1[:]))
                step.then(dve.bn_aggr(hstat[:], hparts[:]))
                dve.tensor_scalar(hstd[:], hstat[:, 1:2], EPS, None, ALU.add).then_inc(s_dve, 1)
                dve.wait_ge(s_act, 3)
                step.then(dve.reciprocal(hstd[:], hstd[:]))
                step.then(dve.tensor_scalar(h1[:], h1[:], hstat[:, 0:1], hstd[:], ALU.subtract, ALU.mult))
                step.then(dve.tensor_tensor(h1[:], h1[:], rows8[:, 1, :], ALU.mult))
                step.then(dve.tensor_tensor(h1[:], h1[:], rows8[:, 2, :], ALU.add))
                dve.tensor_scalar(h1[:], h1[:], 0.0, None, ALU.max).then_inc(s_dve, 1)
                dve.wait_ge(s_ps, 5)
                dve.tensor_copy(h1T[:], bank[6][:, 0:XH]).then_inc(s_dve, 1)
                dve.wait_ge(s_ps, 6)
                step.then(dve.tensor_tensor(logits[:], bank[7][0:XH, 0:3], b2_8[:], ALU.add))
                step.then(dve.tensor_reduce(lmax[:], logits[:], AXIS.X, ALU.max))
                dve.tensor_scalar(lmax[:], lmax[:], -1.0, None, ALU.mult).then_inc(s_dve, 1)
                dve.wait_ge(s_act, 6)
                step.then(dve.reciprocal(esum[:], esum[:]))
                dve.tensor_scalar(wts[:], expo[:], esum[:], None, ALU.mult).then_inc(s_dve, 1)
                dve.wait_ge(s_dve, WTS)
                dve.tensor_copy(ww[:], wts[:, 2:3])
                dve.tensor_scalar(diag[:, 0, :], sh.ident[0:XH, 0:XH], wts[:, 0:1], None, ALU.mult)
                dve.tensor_scalar(diag[:, 1, :], sh.ident[0:XH, 0:XH], wts[:, 1:2], None, ALU.mult).then_inc(s_dve, 1)
                dve.wait_ge(s_ps, 7)
                step.then(dve.tensor_tensor(c1[:], bank[4][:, XH:2 * XH], decorr[:], ALU.mult))
                step.then(dve.tensor_tensor(c1[:], bank[4][:, 0:XH], c1[:], ALU.add))


def l0_cross_batches(nc, sh, bank, context, c_stats, c_rstd, wgT, woT, fbias, out_bias, c1, ww):
    SIDES = 2 * TPB
    FRONT = [("X", 0), ("Y", 0)] + [("F", n) for n in range(2 * SIDES)]
    BACK = [("A", n) for n in range(3)] + [("T", 0)] + [("B", n) for n in range(4)] + [("G", n) for n in range(4)] + [
        ("R", 0), ("O", 0)]
    COUNT = {"X": 1, "Y": 1, "F": 8, "A": 3, "T": 1, "B": 4, "G": 4, "R": 1, "O": 1}
    place = {job: n % 8 for n, job in enumerate(FRONT + BACK)}
    assert len(FRONT + BACK) % 8 == 0

    def before(sequence, at):
        job, _ = sequence[at]
        return next(((j, b) for j, b in reversed(sequence[:at]) if place[j] == place[job]), None)

    def sequence(b):
        return [(j, n + d) for n in range(b - 2, b + 1) for jobs, d in ((FRONT, 1), (BACK, 0)) for j in jobs if n + d >= 0
                and n + d < BATCH]

    with ExitStack() as ctx:
        sb, ps, sem = alloc(nc, ctx, "x0b")
        xn = sb("xn", [P, TPB, DIM])
        cn = sb("cn", [P, TPB, DIM])
        xT = sb("xT", [P, KC, SEQ])
        cT = sb("cT", [P, KC, SEQ])
        f = sb("f", [P, 2, SIDES, INNER])
        g = sb("g", [P, 2, TPB, XH, HD + 1])
        sq = sb("sq", [P, SIDES, INNER])
        fsum = sb("fsum", [P, SIDES, XH])
        fsq = sb("fsq", [P, SIDES, XH])
        norm = sb("norm", [P, SIDES, XH])
        rnorm = sb("rnorm", [P, SIDES, XH])
        var = sb("var", [P, SIDES, XH])
        vden = sb("vden", [P, SIDES, XH])
        ratio = sb("ratio", [P, 2, SIDES, XH])
        a_sb = sb("a_sb", [P, XH, HD + 1])
        s_diag = sb("s_diag", [P, XH, XH])
        t_sb = sb("t_sb", [XH, DIM])
        b_sb = sb("b_sb", [P, XH, DIM])
        gT = sb("gT", [P, XH, SEQ])
        rT = sb("rT", [XH, SEQ])
        xsum = sb("xsum", [P, TPB, DIM])
        parts = sb("parts", [P, TPB, 6])
        means = sb("means", [P, TPB, 2])
        filled = {k: sem(f"{k}_filled") for k in COUNT}
        drained = {k: sem(f"{k}_drained") for k in COUNT}
        s_norm, s_sq, s_sqrt, s_g, s_stat, s_f, s_sum, s_zero, s_fsq = (
            sem("tokens_normalised"), sem("squares_ready"), sem("norms_ready"), sem("scaled_ready"), sem("stat_step"),
            sem("front_step"), sem("sum_step"), sem("diag_cleared"), sem("square_sums_ready"))
        F_STEPS = 8

        with nc.Block() as block:

            @block.gpsimd
            def _(pool):
                pool.memset(s_diag[:], 0.0).then_inc(s_zero, 1)

            @block.tensor
            def _(pe):
                def job(kind, n, b, p, prior):
                    if prior:
                        (k0, n0), b0 = prior
                        pe.wait_ge(drained[k0], COUNT[k0] * b0 + n0 + 1)
                    o = bank[place[(kind, n)]]
                    if kind in "XY":
                        if kind == "X":
                            pe.wait_ge(s_norm, b + 1)
                        tokens = xn if kind == "X" else cn
                        for k in range(KC):
                            for t in range(TPB):
                                last = pe.transpose(o[:, k * SEQ + t * P:k * SEQ + (t + 1) * P], tokens[:, t, k * P:(k + 1) * P],
                                                    sh.ident[:])
                    elif kind == "F":
                        side, half = n // 2, n % 2
                        if n % 4 == 0:
                            pe.wait_ge(drained["Y" if n == 0 else "X"], b + 1)
                        src = cT if side < TPB else xT
                        t = side % TPB
                        for k in range(KC):
                            last = pe.matmul(o[:], src[:, k, t * P:(t + 1) * P], wgT[:, k, half * 512:(half + 1) * 512],
                                             start=k == 0, stop=k == KC - 1)
                    elif kind == "A":
                        if n == 0:
                            pe.wait_ge(s_g, b + 1)
                        for i, h in enumerate(range(3 * n, min(3 * n + 3, XH))):
                            for t in range(TPB):
                                last = pe.matmul(o[:, i * (HD + 1):(i + 1) * (HD + 1)], f[:, p, t, h * P:(h + 1) * P],
                                                 g[:, p, t, h, :], start=t == 0, stop=t == TPB - 1)
                    elif kind == "T":
                        pe.wait_ge(drained["A"], 3 * (b + 1))
                        for h in range(XH):
                            last = pe.matmul(o[0:XH, 0:DIM], s_diag[:, h, :], woT[:, h, :], start=h == 0, stop=h == XH - 1)
                    elif kind == "B":
                        for i in range(2):
                            last = pe.matmul(o[:, i * DIM:(i + 1) * DIM], a_sb[:, 2 * n + i, 0:HD], woT[:, 2 * n + i, :],
                                             start=True, stop=True)
                    elif kind == "G":
                        for i in range(2):
                            for t in range(TPB):
                                h = 2 * n + i
                                last = pe.transpose(o[:, i * SEQ + t * P:i * SEQ + (t + 1) * P],
                                                    f[:, p, TPB + t, h * P:(h + 1) * P], sh.ident[:])
                    elif kind == "R":
                        for t in range(TPB):
                            last = pe.transpose(o[0:XH, t * P:(t + 1) * P], ratio[:, p, TPB + t, :], sh.ident[:])
                    elif kind == "O":
                        pe.wait_ge(drained["B"], 4 * (b + 1))
                        pe.wait_ge(drained["G"], 4 * (b + 1))
                        pe.wait_ge(drained["R"], b + 1)
                        for t in range(TPB):
                            for h in range(XH):
                                pe.matmul(o[:, t * DIM:(t + 1) * DIM], gT[:, h, t * P:(t + 1) * P], b_sb[:, h, :],
                                          start=h == 0, stop=False)
                            last = pe.matmul(o[:, t * DIM:(t + 1) * DIM], rT[:, t * P:(t + 1) * P], t_sb[:], start=False,
                                             stop=True)
                    last.then_inc(filled[kind], 1)

                def jobs(which, b, p, turn):
                    seq = sequence(turn)
                    own = turn + 1 if which is FRONT else turn
                    for kind, n in which:
                        prior = before(seq, seq.index(((kind, n), own)))
                        pe_prior = None
                        if prior:
                            pe_prior = (prior[0], b + (prior[1] - own))
                        job(kind, n, b, p, pe_prior)

                jobs(FRONT, 0, 0, -1)
                for b in range(2):
                    jobs(FRONT, b + 1, 1 - b, b)
                    jobs(BACK, b, b, b)
                with pe.Fori(1, BATCH // 2 - 1) as pair:
                    for p in range(2):
                        jobs(FRONT, 2 * pair + (p + 1), 1 - p, 5)
                        jobs(BACK, 2 * pair + p, p, 5)
                jobs(FRONT, BATCH - 1, 1, BATCH - 2)
                jobs(BACK, BATCH - 2, 0, BATCH - 2)
                jobs(BACK, BATCH - 1, 1, BATCH - 1)

            @block.scalar
            def _(act):
                def front(b, p):
                    for kind, dst in (("X", xT), ("Y", cT)):
                        act.wait_ge(filled[kind], b + 1)
                        act.copy(dst[:].rearrange("p k s -> p (k s)"), bank[place[(kind, 0)]][:]).then_inc(drained[kind], 1)
                    wait_past(act, s_fsq, b)
                    for side in range(SIDES):
                        act.wait_ge(drained["F"], 8 * b + 2 * side + 2)
                        act.activation(sq[:, side, :], f[:, p, side, :], ACT.Square).then_inc(s_sq, 1)

                def norms(b):
                    act.wait_ge(s_fsq, b + 1)
                    act.activation(norm[:], fsq[:], ACT.Sqrt).then_inc(s_sqrt, 1)

                def back(b, p, after):
                    for n in range(3):
                        act.wait_ge(filled["A"], 3 * b + n + 1)
                        heads = min(3, XH - 3 * n)
                        o = bank[place[("A", n)]][:, 0:heads * (HD + 1)].rearrange("p (h d) -> p h d", d=HD + 1)
                        act.copy(a_sb[:, 3 * n:3 * n + heads, :], o)
                        last = act.copy(s_diag[:].rearrange("p a b -> p (a b)")[:, 3 * n * (XH + 1):][:, 0:(heads - 1) * (XH + 1) + 1:XH + 1],
                                        o[:, :, HD])
                        last.then_inc(drained["A"], 1)
                    act.wait_ge(filled["T"], b + 1)
                    act.activation(t_sb[:], bank[place[("T", 0)]][0:XH, 0:DIM], ACT.Copy, scale=ww[:]).then_inc(drained["T"], 1)
                    for n in range(4):
                        act.wait_ge(filled["B"], 4 * b + n + 1)
                        for i in range(2):
                            h = 2 * n + i
                            last = act.activation(b_sb[:, h, :], bank[place[("B", n)]][:, i * DIM:(i + 1) * DIM], ACT.Copy,
                                                  scale=c1[:, h:h + 1])
                        last.then_inc(drained["B"], 1)
                    if after is not None:
                        norms(after)
                    for n in range(4):
                        act.wait_ge(filled["G"], 4 * b + n + 1)
                        act.copy(gT[:, 2 * n:2 * n + 2, :].rearrange("p h s -> p (h s)"), bank[place[("G", n)]][:]).then_inc(
                            drained["G"], 1)
                    act.wait_ge(filled["R"], b + 1)
                    act.copy(rT[:], bank[place[("R", 0)]][0:XH, 0:SEQ]).then_inc(drained["R"], 1)

                act.wait_ge(s_zero, 1)
                front(0, 0)
                norms(0)
                for b in range(2):
                    front(b + 1, 1 - b)
                    back(b, b, b + 1)
                with act.Fori(1, BATCH // 2 - 1) as pair:
                    for p in range(2):
                        front(2 * pair + (p + 1), 1 - p)
                        back(2 * pair + p, p, 2 * pair + (p + 1))
                front(BATCH - 1, 1)
                back(BATCH - 2, 0, BATCH - 1)
                back(BATCH - 1, 1, None)

            @block.vector
            def _(dve):
                def normalise(b):
                    for t in range(TPB):
                        tile = TPB * b + t
                        dve.tensor_scalar(xn[:, t, :], sh.x[:, tile, :], sh.stats[:, tile, 0:1], sh.rstd[:, bass.ds(tile, 1)],
                                          ALU.subtract, ALU.mult)
                        ins = dve.tensor_scalar(cn[:, t, :], context[:, tile, :], c_stats[:, tile, 0:1],
                                                c_rstd[:, bass.ds(tile, 1)], ALU.subtract, ALU.mult)
                    ins.then_inc(s_norm, 1)

                def front(b, p):
                    step = Steps(dve, s_f, b * F_STEPS)
                    for n in range(2 * SIDES):
                        side, half = n // 2, n % 2
                        dve.wait_ge(filled["F"], 8 * b + n + 1)
                        dve.tensor_tensor(f[:, p, side, half * 512:(half + 1) * 512], bank[place[("F", n)]][:],
                                          fbias[:, half * 512:(half + 1) * 512], ALU.add).then_inc(drained["F"], 1)
                        if n == 1 and not (isinstance(b, int) and b == BATCH - 1):
                            dve.wait_ge(filled["X"], b + 1)
                            dve.wait_ge(filled["Y"], b + 1)
                            normalise(b + 1)
                    heads = lambda a: a.rearrange("p s (h d) -> p (s h) d", d=HD)
                    flat = lambda a: a.rearrange("p s h -> p (s h)")
                    dve.wait_ge(drained["F"], 8 * (b + 1))
                    dve.tensor_reduce(flat(fsum[:]), heads(f[:, p]), AXIS.X, ALU.add)
                    dve.wait_ge(s_sq, SIDES * (b + 1))
                    dve.tensor_reduce(flat(fsq[:]), heads(sq[:]), AXIS.X, ALU.add).then_inc(s_fsq, 1)
                    dve.wait_ge(s_fsq, b + 1)
                    step.then(dve.tensor_tensor(fsum[:], fsum[:], fsum[:], ALU.mult))
                    step.then(dve.scalar_tensor_tensor(var[:], fsum[:], -1.0 / HD, fsq[:], ALU.mult, ALU.add))
                    step.then(dve.tensor_scalar(var[:], var[:], 1.0 / (HD - 1), None, ALU.mult))
                    step.then(dve.tensor_scalar(vden[:], var[:], 1.0, None, ALU.add))
                    step.then(dve.reciprocal(vden[:], vden[:]))
                    step.then(dve.tensor_scalar(var[:], var[:], 1.0, 2.0, ALU.min, ALU.mult))
                    step.then(dve.tensor_tensor(ratio[:, p], var[:], vden[:], ALU.mult))
                    dve.wait_ge(s_sqrt, b + 1)
                    step.then(dve.reciprocal(rnorm[:], norm[:]))
                    assert step.count == F_STEPS
                    for t in range(TPB):
                        dve.tensor_copy(g[:, p, t, :, HD], ratio[:, p, t, :])
                        dve.tensor_tensor(g[:, p, t, :, 0:HD], f[:, p, t, :].rearrange("p (h d) -> p h d", d=HD),
                                          rnorm[:, t, :].unsqueeze(2).broadcast_to([P, XH, HD]), ALU.mult)
                        fq = f[:, p, TPB + t, :].rearrange("p (h d) -> p h d", d=HD)
                        last = dve.tensor_tensor(fq, fq, rnorm[:, TPB + t, :].unsqueeze(2).broadcast_to([P, XH, HD]), ALU.mult)
                    last.then_inc(s_g, 1)

                def back(b, p):
                    o = bank[place[("O", 0)]]
                    dve.wait_ge(filled["O"], b + 1)
                    for t in range(TPB):
                        last = dve.tensor_tensor(xsum[:, t, :], o[:, t * DIM:(t + 1) * DIM], out_bias[:], ALU.add)
                    last.then_inc(drained["O"], 1)
                    dve.wait_ge(drained["O"], b + 1)
                    xb = sh.x[:, bass.ds(TPB * b, TPB), :]
                    dve.tensor_tensor(xb, xb, xsum[:], ALU.add).then_inc(s_sum, 1)
                    wait_apart(dve, s_sum, b + 1, sh.scratch[:])
                    batch_stats(dve, Steps(dve, s_stat, b * STATS_STEPS), sh, b, parts, means[:])

                normalise(0)
                front(0, 0)
                for b in range(2):
                    front(b + 1, 1 - b)
                    back(b, b)
                with dve.Fori(1, BATCH // 2 - 1) as pair:
                    for p in range(2):
                        front(2 * pair + (p + 1), 1 - p)
                        back(2 * pair + p, p)
                front(BATCH - 1, 1)
                back(BATCH - 2, 0)
                back(BATCH - 1, 1)


HEADS = 16


class Piece:

    def __init__(self, kind, number, ahead):
        self.kind, self.number, self.ahead = kind, number, ahead


class Plan:

    def __init__(self, slots, counts, start):
        self.slots = {h: [Piece(*p) for p in pieces] for h, pieces in slots.items()}
        self.counts = counts
        self.start = [Piece(k, n, 0) for k, n in start]
        every = [p for h in range(HEADS) for p in self.slots.get(h, [])]
        self.every = every
        assert len(every) == sum(counts.values()) and len(every) % 2 == 0

    def of_slot(self, h, first, last):
        for p in self.slots.get(h, []):
            if first and p.ahead == 0 and (p.kind, p.number) in {(s.kind, s.number) for s in self.start}:
                continue
            if first and p.ahead < 0 or last and p.ahead > 0:
                continue
            yield p

    def done(self, piece, b):
        return self.counts[piece.kind] * (b + piece.ahead) + piece.number + 1


def heads_attention(nc, sh, name, plan, Wq, Wk, Wv, Wo, dh, scale, biases=None, ctx_in=None, mask=None):
    cross = ctx_in is not None
    pad = max(dh, 32)
    per_chunk = P // pad
    chunks = HEADS // per_chunk
    inner = HEADS * dh
    oc = inner // P
    QH = 4
    quarters = HEADS // QH
    vcols = inner // 2
    O_PER = plan.counts["O"]
    with ExitStack() as ctx:
        sb, ps, sem = alloc(nc, ctx, name)
        wq = sb("wq", [P, KC, chunks * P])
        wk = sb("wk", [P, KC, chunks * P])
        wv = sb("wv", [P, KC, inner])
        wo = sb("wo", [P, oc, DIM])
        obias = sb("obias", [P, DIM])
        kq_bias = sb("kq_bias", [P, 2, chunks])
        if biases:
            bv_col = sb("bv_col", [P, oc])
            bv_wide = sb("bv_wide", [P, oc, P])
        if cross:
            tokens_c = sb("tokens_c", [P, TPB, DIM])
            cT = sb("cT", [P, KC, SEQ])
            mask_all = sb("mask_all", [P, BATCH, SEQ])
            mask_now = sb("mask_now", [P, SEQ])
            score = sb("score", [P, 2, TPB, SEQ])
        xn = sb("xn", [P, TPB, DIM])
        xT = sb("xT", [P, KC, SEQ])
        kT = sb("kT", [P, chunks, SEQ])
        qT = sb("qT", [P, chunks, SEQ])
        v = sb("v", [P, TPB, inner])
        top = sb("top", [P, 2, TPB])
        ntop = sb("ntop", [P, 2, TPB])
        prob = sb("prob", [P, 2, TPB, SEQ])
        den = sb("den", [P, TPB, HEADS])
        rden = sb("rden", [P, 2, TPB, QH])
        pT = sb("pT", [P, 2, TPB, SEQ])
        out = sb("out", [P, TPB, inner])
        outT = sb("outT", [P, oc, SEQ])
        xsum = sb("xsum", [P, TPB, DIM])
        parts = sb("parts", [P, TPB, 6])
        means = sb("means", [P, TPB, 2])
        s_ps = [ps(f"s_ps{n}", [P, TPB, SEQ]) for n in range(2)]
        pT_ps = [ps(f"pT_ps{n}", [P, TPB, SEQ]) for n in range(2)]
        o_ps = [ps(f"o_ps{n}", [P, 512]) for n in range(2)]
        fill = [ps(f"fill{n}", [P, 512]) for n in range(2)]

        s_w, s_b, s_prep, s_bias = sem("weights_loaded"), sem("biases_loaded"), sem("prepared"), sem("bias_in_psum")
        s_ctx, s_col = sem("context_loaded"), sem("bias_columns_loaded")
        s_xn = sem("xn_ready")
        filled = {k: sem(f"{k}_filled") for k in plan.counts}
        drained = {k: sem(f"{k}_drained") for k in plan.counts}
        s_sc, s_top, s_prob = sem("scores_in_psum"), sem("top_ready"), sem("probs_ready")
        s_pTp, s_pT, s_op, s_out = sem("pT_in_psum"), sem("pT_ready"), sem("quarter_in_psum"), sem("quarter_ready")
        s_max, s_rden, s_sum, s_stat = sem("max_step"), sem("rden_step"), sem("sum_step"), sem("stat_step")
        s_mask = sem("mask_step")

        with nc.Block() as block:

            @block.sync
            def _(sp):
                if dh == pad:
                    sp.dma_start(wq[:], rows(Wq)).then_inc(s_w, 16)
                    sp.dma_start(wk[:], rows(Wk)).then_inc(s_w, 16)
                else:
                    sp.wait_ge(s_prep, 2)
                    for w, W in ((wq, Wq), (wk, Wk)):
                        for k in range(KC):
                            sp.dma_start(w[:, k].rearrange("p (h e) -> p h e", e=pad)[:, :, 0:dh],
                                         W[k * P:(k + 1) * P, :].rearrange("p (h e) -> p h e", e=dh)).then_inc(s_w, 16)
                sp.dma_start(wv[:], rows(Wv)).then_inc(s_w, 16)
                sp.dma_start(wo[:], rows(Wo)).then_inc(s_w, 16)
                if biases:
                    sp.dma_start(obias[:], broadcast_row(biases["bo"])).then_inc(s_b, 16)
                if cross:
                    sp.dma_start(mask_all[:].rearrange("p b s -> p (b s)"),
                                 broadcast_row(mask.rearrange("b u v s -> (b u v s)"))).then_inc(s_b, 16)

            @block.gpsimd
            def _(pool):
                if dh != pad:
                    pool.memset(wq[:], 0.0).then_inc(s_prep, 1)
                    pool.memset(wk[:], 0.0).then_inc(s_prep, 1)

            @block.scalar
            def _(act):
                if biases:
                    with nc.allow_non_contiguous_dma("bias columns"):
                        for col, b in ((kq_bias[:, 0, :], biases["bk"]), (kq_bias[:, 1, :], biases["bq"]), (bv_col[:], biases["bv"])):
                            act.dma_start(col, b.rearrange("(c p) -> p c", p=P)).then_inc(s_col, 16)

            W_LOADS = 16 * (4 if dh == pad else 2 + 2 * KC)

            @block.vector
            def _(dve):
                if biases:
                    dve.wait_ge(s_col, 48)
                    dve.wait_ge(s_b, 16)
                    dve.tensor_scalar(kq_bias[:, 1, :], kq_bias[:, 1, :], scale, None, ALU.mult).then_inc(s_prep, 1)
                    for c in range(oc):
                        dve.tensor_scalar(bv_wide[:, c, :], sh.ones[:], bv_col[:, c:c + 1], None, ALU.mult).then_inc(s_prep, 1)
                    dve.wait_ge(s_bias, 1)
                    dve.tensor_tensor(obias[:], fill[0][:, 0:DIM], obias[:], ALU.add).then_inc(s_prep, 1)
                    dve.wait_ge(s_prep, 2 + oc)
                dve.wait_ge(s_w, W_LOADS)
                if cross:
                    dve.wait_ge(s_b, 16)

            @block.tensor
            def _(pe):
                if biases:
                    pe.wait_ge(s_w, W_LOADS)
                    pe.wait_ge(s_prep, 1 + oc)
                    for c in range(oc):
                        last = pe.matmul(fill[0][:, 0:DIM], bv_wide[:, c, :], wo[:, c, :], start=c == 0, stop=c == oc - 1)
                    last.then_inc(s_bias, 1)

        def over_batches(engine, slot):
            for h in range(HEADS):
                slot(0, h, True, False)
            with engine.Fori(1, BATCH - 1) as b:
                for h in range(HEADS):
                    slot(b, h, False, False)
            for h in range(HEADS):
                slot(BATCH - 1, h, False, True)

        order = {}
        n = 0
        for p in plan.start:
            order[("start", p.kind, p.number)] = n
            n += 1
        for h in range(HEADS):
            for p in plan.of_slot(h, True, False):
                order[("first", p.kind, p.number)] = n
                n += 1
        assert n % 2 == 0
        for i, p in enumerate(plan.every):
            order[("loop", p.kind, p.number)] = i
        tail = 0
        for h in range(HEADS):
            for p in plan.of_slot(h, False, True):
                order[("last", p.kind, p.number)] = tail
                tail += 1
        ends = [p for h in range(HEADS) for p in plan.slots.get(h, []) if p.ahead < 0]
        ends = [Piece(p.kind, p.number, 0) for p in ends]
        for p in ends:
            order[("end", p.kind, p.number)] = tail
            tail += 1
        before = {}
        seq = [("start", p, 0) for p in plan.start]
        seq += [("first", p, 0) for h in range(HEADS) for p in plan.of_slot(h, True, False)]
        for i, (w, p, b) in enumerate(seq):
            before[(w, p.kind, p.number)] = (seq[i - 2][1], 0) if i >= 2 else None
        first2 = [q for w, q, b in seq[-2:]]
        for i, p in enumerate(plan.every):
            q = plan.every[i - 2]
            before[("loop", p.kind, p.number)] = (q, 0 if i >= 2 else -1)
        lasts = [p for h in range(HEADS) for p in plan.of_slot(h, False, True)]
        for i, p in enumerate(lasts + ends):
            q = (lasts + ends)[i - 2] if i >= 2 else plan.every[i - 2]
            before[("last" if i < len(lasts) else "end", p.kind, p.number)] = (q, 0 if i >= 2 else -1)

        with nc.Block() as block:

            @block.tensor
            def _(pe):
                def piece(p, b, where):
                    bank = fill[order[(where, p.kind, p.number)] % 2]
                    prior = before[(where, p.kind, p.number)]
                    if prior:
                        q, back = prior
                        pe.wait_ge(drained[q.kind], plan.done(q, b + back))
                    own = b + p.ahead
                    if p.kind in "XY":
                        if p.kind == "X":
                            pe.wait_ge(s_xn, own + 1)
                        else:
                            pe.wait_ge(s_ctx, 16 * (own + 1))
                        tokens = xn if p.kind == "X" else tokens_c
                        for k in range(KC):
                            for t in range(TPB):
                                last = pe.transpose(bank[:, k * SEQ + t * P:k * SEQ + (t + 1) * P],
                                                    tokens[:, t, k * P:(k + 1) * P], sh.ident[:])
                    elif p.kind == "C":
                        pe.wait_ge(drained["X"], own + 1)
                        if cross:
                            pe.wait_ge(drained["Y"], own + 1)
                        c = p.number
                        for side, (w, src) in enumerate(((wk, cT if cross else xT), (wq, xT))):
                            for k in range(KC):
                                last = pe.matmul(bank[:, side * SEQ:(side + 1) * SEQ], w[:, k, c * P:(c + 1) * P],
                                                 src[:, k, :], start=k == 0, stop=k == KC - 1)
                    elif p.kind == "V":
                        src = cT if cross else xT
                        pe.wait_ge(drained["Y" if cross else "X"], own + 1)
                        parts_of = plan.counts["V"] // 2
                        half, t0 = p.number // parts_of, p.number % parts_of
                        for t in ([t0] if parts_of == TPB else range(TPB)):
                            at = 0 if parts_of == TPB else t * vcols
                            for k in range(KC):
                                last = pe.matmul(bank[:, at:at + vcols], src[:, k, t * P:(t + 1) * P],
                                                 wv[:, k, half * vcols:(half + 1) * vcols], start=k == 0, stop=k == KC - 1)
                    elif p.kind == "O":
                        pe.wait_ge(s_out, quarters * own + (quarters // O_PER) * (p.number + 1))
                        for c in range(oc // O_PER):
                            for t in range(TPB):
                                last = pe.transpose(bank[:, c * SEQ + t * P:c * SEQ + (t + 1) * P],
                                                    out[:, t, (p.number * (oc // O_PER) + c) * P:][:, 0:P], sh.ident[:])
                    elif p.kind == "W":
                        pe.wait_ge(drained["O"], O_PER * (own + 1))
                        for t in range(TPB):
                            for c in range(oc):
                                last = pe.matmul(bank[:, t * DIM:(t + 1) * DIM], outT[:, c, t * P:(t + 1) * P], wo[:, c, :],
                                                 start=c == 0, stop=c == oc - 1)
                    last.then_inc(filled[p.kind], 1)

                def scores(b, h):
                    pe.wait_ge(drained["C"], chunks * b + h // per_chunk + 1)
                    r, c = pad * (h % per_chunk), h // per_chunk
                    for t in range(TPB):
                        last = pe.matmul(s_ps[h % 2][:, t, :], qT[r:r + pad, c, t * P:(t + 1) * P], kT[r:r + pad, c, :],
                                         start=True, stop=True)
                    last.then_inc(s_sc, 1)

                def turn(b, h):
                    pe.wait_ge(s_prob, HEADS * b + h + 1)
                    for j in range(TPB):
                        for t in range(TPB):
                            last = pe.transpose(pT_ps[h % 2][:, j, t * P:(t + 1) * P], prob[:, h % 2, t, j * P:(j + 1) * P],
                                                sh.ident[:])
                    last.then_inc(s_pTp, 1)

                def attend(b, h):
                    pe.wait_ge(s_pT, HEADS * b + h + 1)
                    if h % (HEADS // 2) == 0:
                        pe.wait_ge(drained["V"], plan.counts["V"] * b + plan.counts["V"] // 2 * (h // (HEADS // 2) + 1))
                    q = h // QH
                    if h % QH == 0:
                        wait_past(pe, s_out, quarters * b + q - 1)
                    for t in range(TPB):
                        at = (t * QH + h % QH) * dh
                        for j in range(TPB):
                            last = pe.matmul(o_ps[q % 2][:, at:at + dh], pT[:, h % 2, j, t * P:(t + 1) * P],
                                             v[:, j, h * dh:(h + 1) * dh], start=j == 0, stop=j == TPB - 1)
                    if h % QH == QH - 1:
                        last.then_inc(s_op, 1)

                def slot(b, h, first, last):
                    scores(b, h)
                    for p in plan.of_slot(h, first, last):
                        piece(p, b, "first" if first else "last" if last else "loop")
                    for do, lag in ((turn, 1), (attend, 2)):
                        if h >= lag:
                            do(b, h - lag)
                        elif not first:
                            do(b - 1, HEADS + h - lag)

                for p in plan.start:
                    piece(p, 0, "start")
                over_batches(pe, slot)
                turn(BATCH - 1, HEADS - 1)
                attend(BATCH - 1, HEADS - 2)
                attend(BATCH - 1, HEADS - 1)
                for p in ends:
                    piece(p, BATCH - 1, "end")

            @block.scalar
            def _(act):
                def drain(p, b, where):
                    bank = fill[order[(where, p.kind, p.number)] % 2]
                    if p.kind in "XY":
                        act.wait_ge(filled[p.kind], plan.done(p, b))
                        dst = xT if p.kind == "X" else cT
                        act.copy(dst[:].rearrange("p k s -> p (k s)"), bank[:]).then_inc(drained[p.kind], 1)
                    elif p.kind == "C":
                        c = p.number
                        act.wait_ge(filled["C"], plan.done(p, b))
                        if biases:
                            act.activation(kT[:, c, :], bank[:, 0:SEQ], ACT.Identity, bias=kq_bias[:, 0, c:c + 1])
                            act.activation(qT[:, c, :], bank[:, SEQ:2 * SEQ], ACT.Identity, bias=kq_bias[:, 1, c:c + 1],
                                           scale=scale).then_inc(drained["C"], 1)
                        else:
                            act.copy(kT[:, c, :], bank[:, 0:SEQ])
                            act.activation(qT[:, c, :], bank[:, SEQ:2 * SEQ], ACT.Copy, scale=scale).then_inc(drained["C"], 1)

                def slot(b, h, first, last):
                    act.wait_ge(s_top, HEADS * b + h + 1)
                    for t in range(TPB):
                        src = score[:, h % 2, t, :] if cross else s_ps[h % 2][:, t, :]
                        ins = act.activation(prob[:, h % 2, t, :], src, ACT.Exp, bias=ntop[:, h % 2, t:t + 1],
                                             accum_out=den[:, t, h:h + 1])
                    ins.then_inc(s_prob, 1)
                    for p in plan.of_slot(h, first, last):
                        drain(p, b, "first" if first else "last" if last else "loop")

                for p in plan.start:
                    drain(p, 0, "start")
                over_batches(act, slot)

            @block.vector
            def _(dve):
                def normalise(b):
                    for t in range(TPB):
                        ins = dve.tensor_scalar(xn[:, t, :], sh.x[:, TPB * b + t, :], sh.stats[:, TPB * b + t, 0:1],
                                                sh.rstd[:, bass.ds(TPB * b + t, 1)], ALU.subtract, ALU.mult)
                    ins.then_inc(s_xn, 1)

                def maximum(b, h):
                    s = h % 2
                    if cross:
                        wait_apart(dve, s_sc, HEADS * b + h + 1, sh.scratch[:])
                        for t in range(TPB):
                            ins = dve.tensor_tensor_reduce(score[:, s, t, :], s_ps[s][:, t, :], mask_now[:], 1.0, -3e38, ALU.add,
                                                           ALU.max, top[:, s, t:t + 1])
                        ins.then_inc(s_max, 1)
                    else:
                        dve.wait_ge(s_sc, HEADS * b + h + 1)
                        dve.tensor_reduce(top[:, s, :], s_ps[s][:], AXIS.X, ALU.max).then_inc(s_max, 1)
                    dve.wait_ge(s_max, HEADS * b + h + 1)
                    dve.tensor_scalar(ntop[:, s, :], top[:, s, :], -1.0, None, ALU.mult).then_inc(s_top, 1)

                def take_turned(b, h):
                    dve.wait_ge(s_pTp, HEADS * b + h + 1)
                    dve.tensor_copy(pT[:, h % 2], pT_ps[h % 2][:]).then_inc(s_pT, 1)

                def take_quarter(b, q):
                    n = quarters * b + q + 1
                    dve.wait_ge(s_op, n)
                    dve.reciprocal(rden[:, q % 2], den[:, :, q * QH:(q + 1) * QH]).then_inc(s_rden, 1)
                    dve.wait_ge(s_rden, n)
                    for t in range(TPB):
                        src = o_ps[q % 2][:, t * QH * dh:(t + 1) * QH * dh].rearrange("p (h d) -> p h d", d=dh)
                        dst = out[:, t, q * QH * dh:(q + 1) * QH * dh].rearrange("p (h d) -> p h d", d=dh)
                        ins = dve.tensor_tensor(dst, src, rden[:, q % 2, t, :].unsqueeze(2).broadcast_to([P, QH, dh]), ALU.mult)
                    ins.then_inc(s_out, 1)

                def drain(p, b, where):
                    bank = fill[order[(where, p.kind, p.number)] % 2]
                    if p.kind in "XYC":
                        return
                    dve.wait_ge(filled[p.kind], plan.done(p, b))
                    if p.kind == "V":
                        parts_of = plan.counts["V"] // 2
                        half, t0 = p.number // parts_of, p.number % parts_of
                        if parts_of == TPB:
                            dst, src = v[:, t0, half * vcols:(half + 1) * vcols], bank[:, 0:vcols]
                        else:
                            dst = v[:, :, half * vcols:(half + 1) * vcols]
                            src = bank[:, 0:TPB * vcols].rearrange("p (t n) -> p t n", t=TPB)
                        dve.tensor_copy(dst, src).then_inc(drained["V"], 1)
                    elif p.kind == "O":
                        n = oc // O_PER
                        dve.tensor_copy(outT[:, p.number * n:(p.number + 1) * n, :].rearrange("p c s -> p (c s)"),
                                        bank[:, 0:n * SEQ]).then_inc(drained["O"], 1)
                    elif p.kind == "W":
                        own = b + p.ahead
                        if biases:
                            for t in range(TPB):
                                ins = dve.tensor_tensor(xsum[:, t, :], bank[:, t * DIM:(t + 1) * DIM], obias[:], ALU.add)
                            ins.then_inc(drained["W"], 1)
                            dve.wait_ge(drained["W"], own + 1)
                            src = xsum[:].rearrange("p t d -> p (t d)")
                        else:
                            src = bank[:]
                        xb = sh.x[:, bass.ds(TPB * own, TPB), :].rearrange("p t d -> p (t d)")
                        ins = dve.tensor_tensor(xb, xb, src, ALU.add)
                        summed = s_sum if biases else drained["W"]
                        ins.then_inc(summed, 1)
                        wait_apart(dve, summed, own + 1, sh.scratch[:])
                        step = Steps(dve, s_stat, own * STATS_STEPS)
                        batch_stats(dve, step, sh, own, parts, means[:])
                        assert step.count == STATS_STEPS

                def slot(b, h, first, last):
                    if cross and h == 0:
                        dve.tensor_scalar(mask_now[:], mask_all[:, b, :], -1e9, None, ALU.mult).then_inc(s_mask, 1)
                        dve.wait_ge(s_mask, b + 1)
                    maximum(b, h)
                    for p in plan.of_slot(h, first, last):
                        drain(p, b, "first" if first else "last" if last else "loop")
                    if h >= 1:
                        take_turned(b, h - 1)
                    elif not first:
                        take_turned(b - 1, HEADS - 1)
                    if h >= 2 and (h - 2) % QH == QH - 1:
                        take_quarter(b, (h - 2) // QH)
                    elif h == 1 and not first:
                        take_quarter(b - 1, quarters - 1)
                    if h == 2 and not last:
                        dve.wait_ge(filled["X"], b + 1)
                        normalise(b + 1)

                normalise(0)
                for p in plan.start:
                    drain(p, 0, "start")
                over_batches(dve, slot)
                take_turned(BATCH - 1, HEADS - 1)
                take_quarter(BATCH - 1, quarters - 1)
                for p in ends:
                    drain(p, BATCH - 1, "end")

            if cross:
                @block.sync
                def _(sp):
                    tokens = ctx_in.rearrange("b (t p) d -> p (b t) d", p=P)
                    sp.dma_start(tokens_c[:], tokens[:, 0:TPB, :]).then_inc(s_ctx, 16)
                    with sp.Fori(1, BATCH) as b:
                        sp.wait_ge(filled["Y"], b)
                        sp.dma_start(tokens_c[:], tokens[:, bass.ds(TPB * b, TPB), :]).then_inc(s_ctx, 16)


SELF_PLAN = Plan(
    slots={0: [("C", 7, 0)], 2: [("V", 2, 0)], 3: [("V", 3, 0), ("O", 3, -1)], 4: [("X", 0, 1), ("W", 0, -1)],
           5: [("C", 0, 1)], 6: [("C", 1, 1)], 7: [("O", 0, 0)], 8: [("C", 2, 1)], 9: [("C", 3, 1)],
           10: [("V", 0, 1)], 11: [("V", 1, 1), ("O", 1, 0)], 12: [("C", 4, 1)], 13: [("C", 5, 1)], 14: [("C", 6, 1)],
           15: [("O", 2, 0)]},
    counts={"X": 1, "C": 8, "V": 4, "O": 4, "W": 1},
    start=[("X", 0)] + [("C", n) for n in range(8)] + [("V", n) for n in range(4)],
)
CROSS_PLAN = Plan(
    slots={0: [("C", 3, 0)], 2: [("V", 1, 0)], 3: [("X", 0, 1), ("O", 0, -1)], 4: [("Y", 0, 1), ("W", 0, -1)],
           6: [("C", 0, 1)], 8: [("C", 1, 1)], 10: [("V", 0, 1)], 12: [("C", 2, 1)]},
    counts={"X": 1, "Y": 1, "C": 4, "V": 2, "O": 1, "W": 1},
    start=[("X", 0), ("Y", 0)] + [("C", n) for n in range(4)] + [("V", n) for n in range(2)],
)


def l1_attention(nc, sh, Wq, bq, Wk, bk, Wv, bv, Wo, bo):
    heads_attention(nc, sh, "a1", SELF_PLAN, Wq, Wk, Wv, Wo, 64, 64 ** -0.5, biases=dict(bq=bq, bk=bk, bv=bv, bo=bo))


def l1_cross_attention(nc, sh, ctx_in, mask, Wq, Wk, Wv, Wo):
    heads_attention(nc, sh, "x1", CROSS_PLAN, Wq, Wk, Wv, Wo, 16, 16 ** -0.5, ctx_in=ctx_in, mask=mask)


def doubling_sum(dve, step, src, spare, axis_slice, count):
    a, b = src, spare
    shift = 1
    while shift < count:
        dve.tensor_copy(axis_slice(b, 0, shift), axis_slice(a, 0, shift))
        step.then(dve.tensor_tensor(axis_slice(b, shift, count), axis_slice(a, shift, count),
                                    axis_slice(a, 0, count - shift), ALU.add))
        a, b = b, a
        shift *= 2
    return a


def route(nc, sh, name, experts, top_k, tiles, gate_w, gate_b, slots, weights, table, chosen):
    E, K = experts, top_k
    with ExitStack() as ctx:
        sb, ps, sem = alloc(nc, ctx, name)
        gw = sb("gw", [E, DIM])
        gwT = sb("gwT", [P, KC, E])
        gb = sb("gb", [P, E])
        xn = sb("xn", [P, 2, TPB, DIM])
        xT = sb("xT", [P, 2, KC, SEQ])
        logits = sb("logits", [P, TILES, E])
        best = sb("best", [P, TILES, 8])
        best_at = sb("best_at", [P, TILES, 8], U32)
        expert = sb("expert", [P, TILES, 8])
        pick = [chosen if chosen is not None else sb("pick0", [P, TILES, E])] + [sb(f"pick{j}", [P, TILES, E]) for j in range(1, K)]
        both = sb("both", [P, TILES, E]) if K > 1 else pick[0]
        iota_e = sb("iota_e", [P, E])
        before = sb("before", [P, P])
        totals = sb("totals", [P, TILES, E])
        spare = sb("spare", [P, TILES, E])
        need = sb("need", [P, E])
        need2 = sb("need2", [P, E])
        need3 = sb("need3", [P, E])
        steps32 = sb("steps32", [P, TILES])
        over = sb("over", [P, E, TILES])
        slot_f = sb("slot_f", [P, K, TILES])
        iota_t = sb("iota_t", [1, tiles])
        past = sb("past", [1, tiles, E])
        table_f = sb("table_f", [1, tiles])
        if K > 1:
            expo = sb("expo", [P, TILES, E])
            esum = sb("esum", [P, TILES])
            wsum = sb("wsum", [P, TILES])
        NB = TILES * E // 512 or 1
        NW = min(512, TILES * E)
        t_ps = [ps(f"t_ps{n}", [P, 512]) for n in range(2)]
        l_ps = [ps(f"l_ps{n}", [P, 512]) for n in range(2)]
        c_ps = [ps(f"c_ps{n}", [P, 512]) for n in range(4)]
        s_w, s_const, s_n, s_tp, s_t, s_lp, s_l = (sem("weights_loaded"), sem("constants"), sem("normalised"), sem("turned_in_psum"),
                                                    sem("turned"), sem("logits_in_psum"), sem("logits_ready"))
        s_dve, s_cp, s_act, s_pick = sem("dve_step"), sem("counts_in_psum"), sem("exp_ready"), sem("picks_ready")
        s_zero, s_neg = sem("zeroed"), sem("shifted")

        with nc.Block() as block:

            @block.sync
            def _(sp):
                sp.dma_start(gw[:], gate_w).then_inc(s_w, 16)
                sp.dma_start(gb[:], broadcast_row(gate_b)).then_inc(s_w, 16)

            @block.gpsimd
            def _(pool):
                exact = dict(allow_small_or_imprecise_dtypes=True)
                pool.iota(iota_e[:], [[1, E]], base=0, channel_multiplier=0, **exact).then_inc(s_const, 1)
                pool.iota(steps32[:], [[P, TILES]], base=0, channel_multiplier=0, **exact).then_inc(s_const, 1)
                pool.iota(iota_t[:], [[1, tiles]], base=0, channel_multiplier=0, **exact).then_inc(s_const, 1)
                pool.memset(before[:], 1.0).then_inc(s_zero, 1)
                pool.wait_ge(s_zero, 1)
                pool.affine_select(out=before[:], in_=before[:], compare_op=ALU.is_gt, fill=0.0, base=0, pattern=[[1, P]],
                                   channel_multiplier=-1).then_inc(s_const, 1)

            @block.tensor
            def _(pe):
                pe.wait_ge(s_w, 32)
                for k in range(KC):
                    last = pe.transpose(c_ps[0][:, k * E:(k + 1) * E], gw[:, k * P:(k + 1) * P], sh.ident[0:E, 0:E])
                last.then_inc(s_cp, 1)

                def turn(b, p):
                    pe.wait_ge(s_n, b + 1)
                    wait_past(pe, s_t, b - 1)
                    for k in range(KC):
                        for t in range(TPB):
                            last = pe.transpose(t_ps[p][:, k * SEQ + t * P:k * SEQ + (t + 1) * P], xn[:, p, t, k * P:(k + 1) * P],
                                                sh.ident[:])
                    last.then_inc(s_tp, 1)

                def gate(b, p):
                    pe.wait_ge(s_t, b + 1)
                    wait_past(pe, s_l, b - 1)
                    for t in range(TPB):
                        for k in range(KC):
                            last = pe.matmul(l_ps[p][:, t * E:(t + 1) * E], xT[:, p, k, t * P:(t + 1) * P], gwT[:, k, :],
                                             start=k == 0, stop=k == KC - 1)
                    last.then_inc(s_lp, 1)

                pe.wait_ge(s_dve, 1)
                pipelined(pe, turn, gate)
                pe.wait_ge(s_const, 4)
                pe.wait_ge(s_pick, 1)
                flat = both[:].rearrange("p t e -> p (t e)")
                for n in range(NB):
                    last = pe.matmul(c_ps[n][:, 0:NW], sh.ones[:], flat[:, n * NW:(n + 1) * NW], start=True, stop=True)
                last.then_inc(s_cp, 1)
                pe.wait_ge(s_dve, 2)
                for n in range(NB):
                    last = pe.matmul(c_ps[n][:, 0:NW], before[:], flat[:, n * NW:(n + 1) * NW], start=True, stop=True)
                last.then_inc(s_cp, 1)

            @block.scalar
            def _(act):
                def turned(b, p):
                    act.wait_ge(s_tp, b + 1)
                    act.copy(xT[:, p].rearrange("p k s -> p (k s)"), t_ps[p][:]).then_inc(s_t, 1)

                pipelined(act, turned, lambda b, p: None)
                if K > 1:
                    act.wait_ge(s_neg, 1)
                    act.activation(expo[:], expo[:], ACT.Exp).then_inc(s_act, 1)
                    act.activation(weights[:].rearrange("p k t -> p (k t)"), weights[:].rearrange("p k t -> p (k t)"),
                                   ACT.Exp).then_inc(s_act, 1)

            @block.vector
            def _(dve):
                dve.wait_ge(s_cp, 1)
                dve.tensor_copy(gwT[:].rearrange("p k e -> p (k e)"), c_ps[0][:, 0:KC * E]).then_inc(s_dve, 1)

                def normalise(b, p):
                    wait_past(dve, s_tp, b - 1)
                    for t in range(TPB):
                        tile = TPB * b + t
                        last = dve.tensor_scalar(xn[:, p, t, :], sh.x[:, tile, :], sh.stats[:, tile, 0:1],
                                                 sh.rstd[:, bass.ds(tile, 1)], ALU.subtract, ALU.mult)
                    last.then_inc(s_n, 1)

                def take(b, p):
                    dve.wait_ge(s_lp, b + 1)
                    dve.tensor_tensor(logits[:, bass.ds(TPB * b, TPB), :], l_ps[p][:, 0:TPB * E].rearrange("p (t e) -> p t e", e=E),
                                      gb[:].unsqueeze(1).broadcast_to([P, TPB, E]), ALU.add).then_inc(s_l, 1)

                pipelined(dve, normalise, take)
                dve.wait_ge(s_l, BATCH)
                own = sem("own_step")
                step = Steps(dve, own)
                for t in range(TILES):
                    last = dve.max(best[:, t, :], logits[:, t, :])
                step.then(last)
                for t in range(TILES):
                    last = dve.max_index(best_at[:, t, :], best[:, t, :], logits[:, t, :])
                step.then(last)
                step.then(dve.tensor_copy(expert[:], best_at[:]))
                dve.wait_ge(s_const, 4)
                for j in range(K):
                    last = dve.tensor_tensor(pick[j][:], iota_e[:].unsqueeze(1).broadcast_to([P, TILES, E]),
                                             expert[:, :, j].unsqueeze(2).broadcast_to([P, TILES, E]), ALU.is_equal)
                if K > 1:
                    step.then(last)
                    last = dve.tensor_tensor(both[:], pick[0][:], pick[1][:], ALU.add)
                last.then_inc(s_pick, 1)
                dve.wait_ge(s_pick, 1)
                if K > 1:
                    dve.tensor_tensor(expo[:], logits[:], best[:, :, 0].unsqueeze(2).broadcast_to([P, TILES, E]), ALU.subtract)
                    dve.tensor_tensor(weights[:], best[:, :, 0:K].rearrange("p t k -> p k t"),
                                      best[:, :, 0].unsqueeze(1).broadcast_to([P, K, TILES]), ALU.subtract).then_inc(s_neg, 1)
                dve.wait_ge(s_cp, 2)
                flat = lambda a: a[:].rearrange("p t e -> p (t e)")
                for n in range(NB):
                    last = dve.tensor_copy(flat(totals)[:, n * NW:(n + 1) * NW], c_ps[n][:, 0:NW])
                step.then(last)
                dve.memset(sh.scratch[:], 0.0).then_inc(s_dve, 1)
                sums = doubling_sum(dve, step, totals, spare, lambda a, i, j: a[:, i:j, :], TILES)
                other = spare if sums is totals else totals
                step.then(dve.tensor_tensor(over[:], sums[:, TILES - 1, :].unsqueeze(2).broadcast_to([P, E, TILES]),
                                            steps32[:].unsqueeze(1).broadcast_to([P, E, TILES]), ALU.is_gt))
                step.then(dve.tensor_reduce(need[:], over[:], AXIS.X, ALU.add))
                step.then(dve.tensor_copy(need3[:], need[:]))
                ends = doubling_sum(dve, step, need3, need2, lambda a, i, j: a[:, i:j], E)
                step.then(dve.tensor_tensor(past[:], iota_t[:].unsqueeze(2).broadcast_to([1, tiles, E]),
                                            ends[0:1, :].unsqueeze(1).broadcast_to([1, tiles, E]), ALU.is_ge))
                step.then(dve.tensor_reduce(table_f[:], past[:], AXIS.X, ALU.add))
                step.then(dve.tensor_scalar(table_f[:], table_f[:], float(E - 1), None, ALU.min))
                dve.tensor_copy(table[:], table_f[:])
                step.then(dve.tensor_tensor(need[:], ends[:], need[:], ALU.subtract))
                step.then(dve.tensor_scalar(need[:], need[:], float(P), None, ALU.mult))
                dve.tensor_copy(other[:, 0, :], need[:])
                step.then(dve.tensor_tensor(other[:, 1:TILES, :], sums[:, 0:TILES - 1, :],
                                            need[:].unsqueeze(1).broadcast_to([P, TILES - 1, E]), ALU.add))
                dve.wait_ge(s_cp, 3)
                for n in range(NB):
                    last = dve.tensor_tensor(flat(other)[:, n * NW:(n + 1) * NW], c_ps[n][:, 0:NW],
                                             flat(other)[:, n * NW:(n + 1) * NW], ALU.add)
                step.then(last)
                for j in range(K):
                    step.then(dve.tensor_tensor(sums[:], other[:], pick[j][:], ALU.mult))
                    step.then(dve.tensor_reduce(slot_f[:, j, :], sums[:], AXIS.X, ALU.add))
                step.then(dve.tensor_copy(slots[:], slot_f[:]))
                if K > 1:
                    dve.wait_ge(s_act, 2)
                    step.then(dve.tensor_reduce(esum[:], expo[:], AXIS.X, ALU.add))
                    step.then(dve.tensor_reduce(wsum[:], weights[:].rearrange("p k t -> p t k"), AXIS.X, ALU.add))
                    step.then(dve.scalar_tensor_tensor(wsum[:], esum[:], 1e-6, wsum[:], ALU.mult, ALU.add))
                    step.then(dve.reciprocal(wsum[:], wsum[:]))
                    step.then(dve.tensor_tensor(weights[:], weights[:], wsum[:].unsqueeze(1).broadcast_to([P, K, TILES]), ALU.mult))


def dispatch_programs(nc, sh, sem, top_k, slots, xs, scratch_tokens, sent_before):
    s_n, s_sent = sem("dispatch_normalised"), sh.sent

    def vector(dve):
        for t in range(TILES):
            n = t % BUFFERS
            if t >= BUFFERS:
                dve.wait_ge(s_sent[n], sent_before + 16 * top_k * (t // BUFFERS))
            dve.tensor_scalar(xs[:, n, :], sh.x[:, t, :], sh.stats[:, t, 0:1], sh.rstd[:, t:t + 1], ALU.subtract,
                              ALU.mult).then_inc(s_n, 1)

    def pool(gp):
        for t in range(TILES):
            gp.wait_ge(s_n, t + 1)
            for j in range(top_k):
                gp.indirect_dma_start(scratch_tokens, bass.IndirectOffsetOnAxis(ap=slots[:, j, t:t + 1], axis=0),
                                      xs[:, t % BUFFERS, :], None).then_inc(s_sent[t % BUFFERS], 16)
        for n in range(BUFFERS):
            gp.wait_ge(s_sent[n], sent_before + 16 * top_k * TILES // BUFFERS)

    return vector, pool


def l0_experts(nc, sh, scratch, gate_w, expert_bias, w_up, w_down):
    E, K, I = 8, 2, 1024
    IC = I // P
    NT = 72
    with ExitStack() as outer:
        sb, ps, sem = alloc(nc, outer, "e0")
        slots = sb("slots", [P, K, TILES], U32)
        weights = sb("weights", [P, K, TILES])
        table = sb("table", [1, NT], I32)
        route(nc, sh, "e0r", E, K, NT, gate_w, expert_bias, slots, weights, table, None)

        with ExitStack() as ctx:
            sb, ps, sem = alloc(nc, ctx, "e0w")
            upT = sb("upT", [P, E, KC, I])
            downT = sb("downT", [P, E, IC, DIM])
            with ExitStack() as prep:
                sb, ps, sem = alloc(nc, prep, "e0p")
                up_nat = sb("up_nat", [P, IC, DIM])
                down_nat = sb("down_nat", [P, KC, I])
                xs = sb("xs", [P, BUFFERS, DIM])
                bank = [ps(f"bank{n}", [P, 512]) for n in range(8)]
                s_up, s_down, s_fill, s_act, s_dve = (sem("up_loaded"), sem("down_loaded"), sem("bank_filled"),
                                                      sem("act_drained"), sem("dve_drained"))
                vector, pool = dispatch_programs(nc, sh, sem, K, slots, xs, scratch.tokens, 0)
                with nc.Block() as block:
                    block.gpsimd(pool)

                    @block.sync
                    def _(sp):
                        for e in range(E):
                            if e:
                                sp.wait_ge(s_fill, 8 * (e - 1) + 4)
                            sp.dma_start(up_nat[:], w_up[e].rearrange("(c p) d -> p c d", p=P)).then_inc(s_up, 16)
                            if e:
                                sp.wait_ge(s_fill, 8 * e)
                            sp.dma_start(down_nat[:], w_down[e].rearrange("(c p) d -> p c d", p=P)).then_inc(s_down, 16)

                    @block.tensor
                    def _(pe):
                        for e in range(E):
                            for k in range(KC):
                                for half in range(2):
                                    n = 2 * k + half
                                    if e:
                                        pe.wait_ge(s_act, 4 * (e - 1) + n + 1)
                                    pe.wait_ge(s_up, 16 * (e + 1))
                                    for c in range(4):
                                        last = pe.transpose(bank[n][:, c * P:(c + 1) * P],
                                                            up_nat[:, half * 4 + c, k * P:(k + 1) * P], sh.ident[:])
                                    last.then_inc(s_fill, 1)
                            for n in range(4):
                                if e:
                                    pe.wait_ge(s_dve, 4 * (e - 1) + n + 1)
                                pe.wait_ge(s_down, 16 * (e + 1))
                                for c in range(2):
                                    for m in range(KC):
                                        last = pe.transpose(bank[4 + n][:, c * DIM + m * P:c * DIM + (m + 1) * P],
                                                            down_nat[:, m, (2 * n + c) * P:(2 * n + c + 1) * P], sh.ident[:])
                                last.then_inc(s_fill, 1)

                    @block.scalar
                    def _(act):
                        for e in range(E):
                            for n in range(4):
                                act.wait_ge(s_fill, 8 * e + n + 1)
                                last = act.copy(upT[:, e, n // 2, n % 2 * 512:(n % 2 + 1) * 512], bank[n][:])
                                last.then_inc(s_act, 1)

                    @block.vector
                    def _(dve):
                        vector(dve)
                        for e in range(E):
                            for n in range(4):
                                dve.wait_ge(s_fill, 8 * e + 4 + n + 1)
                                dve.tensor_copy(downT[:, e, 2 * n:2 * n + 2, :].rearrange("p c d -> p (c d)"),
                                                bank[4 + n][:]).then_inc(s_dve, 1)

            sb, ps, sem = alloc(nc, ctx, "e0x")
            xg = sb("xg", [P, 2, DIM])
            xgT = sb("xgT", [P, 2, KC, P])
            h = sb("h", [P, 2, I])
            hT = sb("hT", [P, 2, IC, P])
            y = sb("y", [P, 2, DIM])
            t_ps = ps("t_ps", [P, 512])
            up_ps = [ps(f"up_ps{n}", [P, 512]) for n in range(2)]
            h_ps = [ps(f"h_ps{n}", [P, 512]) for n in range(2)]
            y_ps = [ps(f"y_ps{n}", [P, 512]) for n in range(2)]
            s_ld = [sem(f"tile_loaded{n}") for n in range(2)]
            s_st = [sem(f"result_stored{n}") for n in range(2)]
            s_tp, s_t, s_upp, s_h, s_hp, s_hT, s_yp, s_y = (sem("x_turned_in_psum"), sem("x_turned"), sem("up_in_psum"),
                                                            sem("gelu_ready"), sem("h_turned_in_psum"), sem("h_turned"),
                                                            sem("y_in_psum"), sem("y_ready"))

            def over_tiles(engine, first, tile):
                if first:
                    first()
                for i in range(2):
                    tile(i, i, False)
                with engine.Fori(1, NT // 2 - 1) as pair:
                    for p in range(2):
                        tile(2 * pair + p, p, False)
                tile(NT - 2, 0, False)
                tile(NT - 1, 1, True)

            with nc.Block() as block:

                @block.sync
                def _(sp):
                    for n in range(2):
                        sp.dma_start(xg[:, n, :], scratch.tokens[n * P:(n + 1) * P, :]).then_inc(s_ld[n], 16)

                    def tile(i, p, last):
                        if not (isinstance(i, int) and i >= NT - 2):
                            sp.wait_ge(s_tp, i + 1)
                            sp.dma_start(xg[:, p, :], scratch.tokens[bass.ds((i + 2) * P, P), :]).then_inc(s_ld[p], 16)
                        sp.wait_ge(s_y, i + 1)
                        sp.dma_start(scratch.results[bass.ds(i * P, P), :], y[:, p, :]).then_inc(s_st[p], 16)

                    over_tiles(sp, None, tile)
                    for n in range(2):
                        sp.wait_ge(s_st[n], 16 * NT // 2)

                @block.tensor
                def _(pe):
                    def turn(i, p, k16):
                        pe.wait_ge(s_ld[p], k16)
                        wait_past(pe, s_t, i)
                        for k in range(KC):
                            last = pe.transpose(t_ps[:, k * P:(k + 1) * P], xg[:, p, k * P:(k + 1) * P], sh.ident[:])
                        last.then_inc(s_tp, 1)

                    def up(i, p):
                        e = pe.value_load(table[0:1, bass.ds(i, 1)], min_val=0, max_val=E - 1)
                        pe.wait_ge(s_t, i + 1)
                        for half in range(2):
                            wait_past(pe, s_h, 2 * i + half - 1)
                            for k in range(KC):
                                last = pe.matmul(up_ps[half][:], xgT[:, p, k, :], upT[:, bass.ds(e, 1), k, half * 512:(half + 1) * 512].rearrange("p a d -> p (a d)"),
                                                 start=k == 0, stop=k == KC - 1)
                            last.then_inc(s_upp, 1)

                    def turn_h(i, p):
                        for half in range(2):
                            pe.wait_ge(s_h, 2 * i + half + 1)
                            wait_past(pe, s_hT, 2 * i + half - 1)
                            for c in range(4):
                                last = pe.transpose(h_ps[half][:, c * P:(c + 1) * P], h[:, p, (half * 4 + c) * P:(half * 4 + c + 1) * P],
                                                    sh.ident[:])
                            last.then_inc(s_hp, 1)

                    def down(i, p):
                        e = pe.value_load(table[0:1, bass.ds(i, 1)], min_val=0, max_val=E - 1)
                        pe.wait_ge(s_hT, 2 * i + 2)
                        wait_past(pe, s_y, i - 1)
                        for c in range(IC):
                            last = pe.matmul(y_ps[p][:, 0:DIM], hT[:, p, c, :], downT[:, bass.ds(e, 1), c, :].rearrange("p a d -> p (a d)"), start=c == 0,
                                             stop=c == IC - 1)
                        last.then_inc(s_yp, 1)

                    def start():
                        turn(0, 0, 16)
                        up(0, 0)

                    def tile(i, p, last):
                        if not last:
                            half = (i + 1) // 2 if isinstance(i, int) else None
                            if isinstance(i, int):
                                turn(i + 1, 1 - p, 16 * ((i + 1) // 2 + 1))
                            else:
                                turn(i + 1, 1 - p, 8 * (i + 1 - (1 - p)) + 16)
                        turn_h(i, p)
                        if not last:
                            up(i + 1, 1 - p)
                        down(i, p)

                    over_tiles(pe, start, tile)

                @block.scalar
                def _(act):
                    def front(i, p):
                        act.wait_ge(s_tp, i + 1)
                        act.copy(xgT[:, p].rearrange("p k s -> p (k s)"), t_ps[:, 0:KC * P]).then_inc(s_t, 1)
                        for half in range(2):
                            act.wait_ge(s_upp, 2 * i + half + 1)
                            act.activation(h[:, p, half * 512:(half + 1) * 512], up_ps[half][:], ACT.Gelu).then_inc(s_h, 1)

                    def tile(i, p, last):
                        if not last:
                            front(i + 1, 1 - p)

                    over_tiles(act, lambda: front(0, 0), tile)

                @block.vector
                def _(dve):
                    def tile(i, p, last):
                        for half in range(2):
                            dve.wait_ge(s_hp, 2 * i + half + 1)
                            dve.tensor_copy(hT[:, p, half * 4:half * 4 + 4, :].rearrange("p c s -> p (c s)"),
                                            h_ps[half][:]).then_inc(s_hT, 1)
                        dve.wait_ge(s_yp, i + 1)
                        if isinstance(i, int):
                            wait_past(dve, s_st[p], 16 * (i // 2))
                        else:
                            dve.wait_ge(s_st[p], 8 * (i - p))
                        dve.tensor_copy(y[:, p, :], y_ps[p][:, 0:DIM]).then_inc(s_y, 1)

                    over_tiles(dve, None, tile)

        l0_experts_combine(nc, sh, scratch, slots, weights, NT)


def l0_experts_combine(nc, sh, scratch, slots, weights, tiles):
    K = 2
    with ExitStack() as ctx:
        sb, ps, sem = alloc(nc, ctx, "e0c")
        ya = sb("ya", [P, BUFFERS, K, DIM])
        out = sb("out", [P, BUFFERS, DIM])
        parts = sb("parts", [P, BUFFERS, 6])
        stat = sb("stat", [P, BUFFERS, 2])
        std = sb("std", [P, BUFFERS])
        r2 = sb("r2", [P, BUFFERS])
        shift = sb("shift", [P, BUFFERS])
        grow = sb("grow", [P, TILES])
        less = sb("less", [P, TILES])
        s_got = sh.got
        s_mix, s_var, s_std, s_own = sem("mixed"), sem("variance_ready"), sem("std_ready"), sem("own_step")
        LAG = 2
        with nc.Block() as block:

            @block.gpsimd
            def _(pool):
                for t in range(TILES):
                    n = t % BUFFERS
                    if t >= BUFFERS:
                        pool.wait_ge(s_mix, t - BUFFERS + 1)
                    for j in range(K):
                        pool.indirect_dma_start(ya[:, n, j, :], None, scratch.results[0:tiles * P, :],
                                                bass.IndirectOffsetOnAxis(ap=slots[:, j, t:t + 1], axis=0)).then_inc(s_got[n], 16)

            @block.scalar
            def _(act):
                for t in range(TILES):
                    n = t % BUFFERS
                    act.wait_ge(s_var, t + 1)
                    act.activation(std[:, n:n + 1], std[:, n:n + 1], ACT.Sqrt).then_inc(s_std, 1)

            @block.vector
            def _(dve):
                step = Steps(dve, s_own)
                step.then(dve.tensor_scalar(grow[:], sh.rstd[:], 1.0, None, ALU.add))
                step.then(dve.tensor_tensor(less[:], sh.stats[:, :, 0], sh.rstd[:], ALU.mult))

                def mix(t):
                    n = t % BUFFERS
                    dve.wait_ge(s_got[n], 16 * K * (t // BUFFERS + 1))
                    step.then(dve.tensor_scalar(out[:, n, :], ya[:, n, 0, :], weights[:, 0, t:t + 1], None, ALU.mult))
                    dve.scalar_tensor_tensor(out[:, n, :], ya[:, n, 1, :], weights[:, 1, t:t + 1], out[:, n, :], ALU.mult,
                                             ALU.add).then_inc(s_mix, 1)
                    dve.wait_ge(s_mix, t + 1)
                    step.then(dve.bn_stats(parts[:, n, :], out[:, n, :]))
                    step.then(dve.bn_aggr(stat[:, n, :], parts[:, n, :]))
                    dve.tensor_scalar(std[:, n:n + 1], stat[:, n, 1:2], EPS, None, ALU.add).then_inc(s_var, 1)

                def add(t):
                    n = t % BUFFERS
                    dve.wait_ge(s_std, t + 1)
                    step.then(dve.reciprocal(r2[:, n:n + 1], std[:, n:n + 1]))
                    step.then(dve.scalar_tensor_tensor(shift[:, n:n + 1], stat[:, n, 0:1], r2[:, n:n + 1], less[:, t:t + 1], ALU.mult,
                                                       ALU.add))
                    step.then(dve.tensor_scalar(sh.x[:, t, :], sh.x[:, t, :], grow[:, t:t + 1], shift[:, n:n + 1], ALU.mult,
                                                ALU.subtract))
                    step.then(dve.scalar_tensor_tensor(sh.x[:, t, :], out[:, n, :], r2[:, n:n + 1], sh.x[:, t, :], ALU.mult,
                                                       ALU.add))
                    token_stats(dve, step, sh, t, parts[:, n, :])

                for t in range(TILES + LAG):
                    if t < TILES:
                        mix(t)
                    if t >= LAG:
                        add(t - LAG)


def l1_experts(nc, sh, scratch, gate_w, gate_b, expert_w, expert_b, result, gathered):
    E, K = 64, 1
    NT = MAX_TILES
    D = 8
    with ExitStack() as outer:
        sb, ps, sem = alloc(nc, outer, "e1")
        slots = sb("slots", [P, K, TILES], U32)
        table = sb("table", [1, NT], I32)
        chosen = sb("chosen", [P, TILES, E])
        eb = sb("eb", [E, DIM])
        route(nc, sh, "e1r", E, K, NT, gate_w, gate_b, slots, None, table, chosen)

        with ExitStack() as ctx:
            sb, ps, sem = alloc(nc, ctx, "e1w")
            ew = sb("ew", [P, E, KC, DIM])
            xs = sb("xs", [P, BUFFERS, DIM])
            s_ew = sem("experts_loaded")
            vector, pool = dispatch_programs(nc, sh, sem, K, slots, xs, scratch.tokens, gathered)
            with nc.Block() as block:
                block.gpsimd(pool)
                block.vector(vector)

                @block.sync
                def _(sp):
                    for e in range(0, E, 8):
                        sp.dma_start(ew[:, e:e + 8].rearrange("p e k d -> p (e k) d"),
                                     expert_w[e:e + 8].rearrange("e (k p) d -> p (e k) d", p=P)).then_inc(s_ew, 16)
                    sp.dma_start(eb[:], expert_b).then_inc(s_ew, 16)
                    sp.wait_ge(s_ew, 16 * 9)

            sb, ps, sem = alloc(nc, ctx, "e1x")
            xg = sb("xg", [P, D, DIM])
            xgT = sb("xgT", [P, 2, KC, P])
            y = sb("y", [P, D, DIM])
            t_ps = [ps(f"t_ps{n}", [P, 512]) for n in range(2)]
            y_ps = [ps(f"y_ps{n}", [P, 512]) for n in range(2)]
            s_ld = [sem(f"tile_loaded{n}") for n in range(D)]
            s_st = [sem(f"result_stored{n}") for n in range(D)]
            s_tp, s_t, s_yp, s_y = sem("x_turned_in_psum"), sem("x_turned"), sem("y_in_psum"), sem("y_ready")

            def over_tiles(engine, tile):
                for i in range(D):
                    tile(i, i, 0)
                with engine.Fori(1, NT // D - 1) as turn:
                    for n in range(D):
                        tile(D * turn + n, n, turn)
                for n in range(D):
                    tile(NT - D + n, n, NT // D - 1)

            with nc.Block() as block:

                @block.sync
                def _(sp):
                    for n in range(D):
                        sp.dma_start(xg[:, n, :], scratch.tokens[n * P:(n + 1) * P, :]).then_inc(s_ld[n], 16)

                    def tile(i, n, turn):
                        if not (isinstance(i, int) and i >= NT - D):
                            sp.wait_ge(s_tp, i + 1)
                            sp.dma_start(xg[:, n, :], scratch.tokens[bass.ds((i + D) * P, P), :]).then_inc(s_ld[n], 16)

                    over_tiles(sp, tile)

                @block.gpsimd
                def _(pool):
                    pass

                @block.tensor
                def _(pe):
                    def turn_x(i, n, turn):
                        pe.wait_ge(s_ld[n], 16 * (turn + 1))
                        wait_past(pe, s_t, i - 1)
                        for k in range(KC):
                            last = pe.transpose(t_ps[n % 2][:, k * P:(k + 1) * P], xg[:, n, k * P:(k + 1) * P], sh.ident[:])
                        last.then_inc(s_tp, 1)

                    def product(i, n):
                        e = pe.value_load(table[0:1, bass.ds(i, 1)], min_val=0, max_val=E - 1)
                        pe.wait_ge(s_t, i + 1)
                        wait_past(pe, s_y, i - 1)
                        for k in range(KC):
                            last = pe.matmul(y_ps[n % 2][:, 0:DIM], xgT[:, n % 2, k, :], ew[:, bass.ds(e, 1), k, :].rearrange("p a d -> p (a d)"), start=k == 0,
                                             stop=k == KC - 1)
                        last.then_inc(s_yp, 1)

                    def tile(i, n, turn):
                        if not (isinstance(i, int) and i == NT - 1):
                            turn_x(i + 1, (n + 1) % D, turn + (1 if n == D - 1 else 0))
                        product(i, n)

                    turn_x(0, 0, 0)
                    over_tiles(pe, tile)

                @block.scalar
                def _(act):
                    def turned(i, n):
                        act.wait_ge(s_tp, i + 1)
                        act.copy(xgT[:, n % 2].rearrange("p k s -> p (k s)"), t_ps[n % 2][:, 0:KC * P]).then_inc(s_t, 1)

                    def tile(i, n, turn):
                        if not (isinstance(i, int) and i == NT - 1):
                            turned(i + 1, (n + 1) % D)
                        act.wait_ge(s_y, i + 1)
                        act.dma_start(scratch.results[bass.ds(i * P, P), :], y[:, n, :]).then_inc(s_st[n], 16)

                    turned(0, 0)
                    over_tiles(act, tile)
                    for n in range(D):
                        act.wait_ge(s_st[n], 16 * NT // D)

                @block.vector
                def _(dve):
                    def tile(i, n, turn):
                        dve.wait_ge(s_yp, i + 1)
                        wait_past(dve, s_st[n], 16 * turn)
                        dve.tensor_copy(y[:, n, :], y_ps[n % 2][:, 0:DIM]).then_inc(s_y, 1)

                    over_tiles(dve, tile)

        with ExitStack() as ctx:
            sb, ps, sem = alloc(nc, ctx, "e1c")
            y = sb("y", [P, BUFFERS, DIM])
            pickT = sb("pickT", [E, 2, P])
            c_ps = [ps(f"c_ps{n}", [P, 512]) for n in range(2)]
            b_ps = [ps(f"b_ps{n}", [P, 512]) for n in range(2)]
            s_got = sh.got
            s_cp, s_c, s_bp, s_sum, s_out = sem("choice_in_psum"), sem("choice_turned"), sem("bias_in_psum"), sem("summed"), sem("stored")
            s_y = sem("result_added")
            dst = result.rearrange("b (t p) d -> p (b t) d", p=P)
            GROUP = 4
            with nc.Block() as block:

                @block.gpsimd
                def _(pool):
                    for t in range(TILES):
                        n = t % BUFFERS
                        if t >= BUFFERS:
                            pool.wait_ge(s_y, t - BUFFERS + 1)
                        pool.indirect_dma_start(y[:, n, :], None, scratch.results,
                                                bass.IndirectOffsetOnAxis(ap=slots[:, 0, t:t + 1], axis=0)).then_inc(s_got[n], 16)

                @block.tensor
                def _(pe):
                    for t in range(TILES):
                        if t >= 2:
                            pe.wait_ge(s_c, t - 1)
                        pe.transpose(c_ps[t % 2][0:E, 0:P], chosen[:, t, :], sh.ident[:]).then_inc(s_cp, 1)
                        if t >= 2:
                            pe.wait_ge(s_sum, t - 1)
                        pe.wait_ge(s_c, t + 1)
                        pe.matmul(b_ps[t % 2][:, 0:DIM], pickT[:, t % 2, :], eb[:], start=True, stop=True).then_inc(s_bp, 1)

                @block.scalar
                def _(act):
                    for t in range(TILES):
                        act.wait_ge(s_cp, t + 1)
                        act.copy(pickT[:, t % 2, :], c_ps[t % 2][0:E, 0:P]).then_inc(s_c, 1)

                @block.vector
                def _(dve):
                    for t in range(TILES):
                        n = t % BUFFERS
                        dve.wait_ge(s_got[n], gathered + 16 * (t // BUFFERS + 1))
                        dve.tensor_tensor(sh.x[:, t, :], sh.x[:, t, :], y[:, n, :], ALU.add).then_inc(s_y, 1)
                        dve.wait_ge(s_y, t + 1)
                        dve.wait_ge(s_bp, t + 1)
                        dve.tensor_tensor(sh.x[:, t, :], sh.x[:, t, :], b_ps[t % 2][:, 0:DIM], ALU.add).then_inc(s_sum, 1)

                @block.sync
                def _(sp):
                    for t in range(0, TILES, GROUP):
                        sp.wait_ge(s_sum, t + GROUP)
                        sp.dma_start(dst[:, t:t + GROUP, :], sh.x[:, t:t + GROUP, :]).then_inc(s_out, 16)
                    sp.wait_ge(s_out, 16 * TILES // GROUP)


def decoder(nc, x, ctx_1024, mask_Bx1x1xS2_fk0, L0_attn_Wq, L0_attn_bq, L0_attn_Wk, L0_attn_bk, L0_attn_Wv, L0_attn_bv,
            L0_attn_Wo, L0_attn_bo, L0_xattn_ln_g, L0_xattn_ln_b, L0_xattn_w_in, L0_xattn_wp_w1, L0_xattn_wp_b1,
            L0_xattn_wp_ln_g, L0_xattn_wp_ln_b, L0_xattn_wp_w2, L0_xattn_wp_b2, L0_xattn_w_out, L0_xattn_b_out,
            L0_ffn_gate_w, L0_ffn_expert_bias, L0_ffn_w_up, L0_ffn_w_down, L1_attn_Wq, L1_attn_bq, L1_attn_Wk, L1_attn_bk,
            L1_attn_Wv, L1_attn_bv, L1_attn_Wo, L1_attn_bo, L1_xattn_Wq, L1_xattn_Wk, L1_xattn_Wv, L1_xattn_Wo,
            L1_ffn_gate_w, L1_ffn_gate_b, L1_ffn_expert_w, L1_ffn_expert_b, result):
    with ExitStack() as ctx:
        sh = Shared(nc, ctx)
        scratch = Sorted(nc)
        s_cleared = ctx.enter_context(nc.semaphore("sorted_tokens_cleared"))
        with ExitStack() as early:
            zeros = early.enter_context(nc.sbuf_tensor("zeros", [P, CLEAR_ROWS // P * DIM], F32))
            load_inputs(nc, sh, x, scratch, zeros, s_cleared)
            norm_scales(nc, sh, "n0")
            l0_attention(nc, sh, L0_attn_Wq, L0_attn_bq, L0_attn_Wk, L0_attn_bk, L0_attn_Wv, L0_attn_bv, L0_attn_Wo,
                         L0_attn_bo, s_cleared)
        clear_semaphores(nc)
        norm_scales(nc, sh, "n1", twice=True)
        l0_cross_attention(nc, sh, ctx_1024, L0_xattn_ln_g, L0_xattn_ln_b, L0_xattn_w_in, L0_xattn_wp_w1, L0_xattn_wp_b1,
                           L0_xattn_wp_ln_g, L0_xattn_wp_ln_b, L0_xattn_wp_w2, L0_xattn_wp_b2, L0_xattn_w_out, L0_xattn_b_out)
        clear_semaphores(nc)
        norm_scales(nc, sh, "n2")
        l0_experts(nc, sh, scratch, L0_ffn_gate_w, L0_ffn_expert_bias, L0_ffn_w_up, L0_ffn_w_down)
        clear_semaphores(nc)
        norm_scales(nc, sh, "n3")
        l1_attention(nc, sh, L1_attn_Wq, L1_attn_bq, L1_attn_Wk, L1_attn_bk, L1_attn_Wv, L1_attn_bv, L1_attn_Wo, L1_attn_bo)
        clear_semaphores(nc)
        norm_scales(nc, sh, "n4")
        l1_cross_attention(nc, sh, ctx_1024, mask_Bx1x1xS2_fk0, L1_xattn_Wq, L1_xattn_Wk, L1_xattn_Wv, L1_xattn_Wo)
        clear_semaphores(nc)
        norm_scales(nc, sh, "n5")
        l1_experts(nc, sh, scratch, L1_ffn_gate_w, L1_ffn_gate_b, L1_ffn_expert_w, L1_ffn_expert_b, result,
                   16 * 2 * TILES // BUFFERS)


_INS = ['x', 'ctx_1024', 'mask_Bx1x1xS2_fk0', 'L0_attn_Wq', 'L0_attn_bq', 'L0_attn_Wk', 'L0_attn_bk', 'L0_attn_Wv',
        'L0_attn_bv', 'L0_attn_Wo', 'L0_attn_bo', 'L0_xattn_ln_g', 'L0_xattn_ln_b', 'L0_xattn_w_in', 'L0_xattn_wp_w1',
        'L0_xattn_wp_b1', 'L0_xattn_wp_ln_g', 'L0_xattn_wp_ln_b', 'L0_xattn_wp_w2', 'L0_xattn_wp_b2', 'L0_xattn_w_out',
        'L0_xattn_b_out', 'L0_ffn_gate_w', 'L0_ffn_expert_bias', 'L0_ffn_w_up', 'L0_ffn_w_down', 'L1_attn_Wq',
        'L1_attn_bq', 'L1_attn_Wk', 'L1_attn_bk', 'L1_attn_Wv', 'L1_attn_bv', 'L1_attn_Wo', 'L1_attn_bo', 'L1_xattn_Wq',
        'L1_xattn_Wk', 'L1_xattn_Wv', 'L1_xattn_Wo', 'L1_ffn_gate_w', 'L1_ffn_gate_b', 'L1_ffn_expert_w',
        'L1_ffn_expert_b']
_OUTS = [((16, 256, 256), 'float32')]


def kernel(**inputs):
    import numpy as _np
    import concourse.bacc as _bacc
    from concourse import mybir as _mybir
    from concourse.bass_utils import run_bass_kernel_spmd as _run

    nc = _bacc.Bacc("TRN2", target_bir_lowering=False, num_devices=1)
    arrays, args = {}, []
    for name in _INS:
        a = _np.ascontiguousarray(inputs[name])
        arrays[f"in_{name}_dram"] = a
        args.append(nc.dram_tensor(f"in_{name}_dram", a.shape, _mybir.dt.from_np(a.dtype), kind="ExternalInput").ap())
    for i, (shape, dtype) in enumerate(_OUTS):
        dt = _mybir.dt.from_np(_np.dtype(dtype))
        args.append(nc.dram_tensor(f"out_{i}_dram", shape, dt, kind="ExternalOutput").ap())
    decoder(nc, *args)
    r = _run(nc, [arrays], core_ids=[0])
    got = tuple(r.results[0][f"out_{i}_dram"] for i in range(len(_OUTS)))
    return got[0]
```
